# Optimizing a Trainium2 kernel written in Bass

```python
import numpy as np
import jax
import jax.numpy as jnp

def _softmax(x, axis=-1):
    return jax.nn.softmax(x, axis=axis)

def _gelu(x):
    return jax.nn.gelu(x, approximate=True)

def _silu(x):
    return jax.nn.silu(x)

def _sigmoid(x):
    return jax.nn.sigmoid(x)

def _layernorm(x, axis=-1, eps=1e-05):
    m = jnp.mean(x, axis=axis, keepdims=True)
    v = jnp.var(x, axis=axis, keepdims=True)
    return (x - m) / jnp.sqrt(v + eps)

def _scatter_add(tgt, idx, src, axis=0):
    return tgt.at[idx].add(src)

def _segment_sum(src, seg, n):
    return jax.ops.segment_sum(src, seg, n)
kernel_name = 'mk_lm_tower_d1_tok_ids256_r4_fd0cd3'

def setup_inputs(seed: int=0):
    np.random.seed(seed)
    _w = jnp.asarray

    def _rec_inputs():
        import jax
        import jax.numpy as jnp
        _rk = jax.random.key(seed)
        x = jax.random.randint(jax.random.fold_in(_rk, 1), (1, 2048), 0, 50257, jnp.int32)
        return x
    x = _rec_inputs()

    def _L0_tok_setup():
        import jax, jax.numpy as jnp
        import numpy as np
        VOCAB = 50257
        DIM = 64

        def _positional_table(seq_len, dim, dtype=jnp.float32):
            pos = jnp.arange(seq_len, dtype=dtype)[:, None]
            d = jnp.arange(dim)
            exponent = (d - d % 2).astype(dtype) / dim
            inv_freq = jnp.power(jnp.asarray(10000.0, dtype), -exponent)
            angle = pos * inv_freq
            return jnp.where(d % 2 == 0, jnp.sin(angle), jnp.cos(angle))
        key = jax.random.key(seed)
        k1, k2 = jax.random.split(key)
        x = jax.random.randint(k1, (32, 1024), 0, VOCAB)
        W = jax.random.normal(k2, (VOCAB, DIM), dtype=jnp.float32)
        return {'x': x, 'W': W}
    _L0_tok_all = _L0_tok_setup()
    _L0_tok_in = {k: v for k, v in _L0_tok_all.items() if k in ('W',)}
    del _L0_tok_all

    def _L0_attn_setup():
        import jax, jax.numpy as jnp
        import numpy as np
        import math
        EMBED_DIM = 64
        SEQ_LEN = 1024
        BATCH = 4
        NUM_SCALES = (24.0, 720.0)
        key = jax.random.key(seed)
        ks = jax.random.split(key, 8)
        d = EMBED_DIM
        x = jax.random.normal(ks[0], (BATCH, SEQ_LEN, d), dtype=jnp.float32)
        s = 1.0 / math.sqrt(d)
        Wq = jax.random.uniform(ks[1], (d, d), jnp.float32, -s, s)
        bq = jax.random.uniform(ks[2], (d,), jnp.float32, -s, s)
        Wk = jax.random.uniform(ks[3], (d, d), jnp.float32, -s, s)
        bk = jax.random.uniform(ks[4], (d,), jnp.float32, -s, s)
        Wv = jax.random.uniform(ks[5], (d, d), jnp.float32, -s, s)
        bv = jax.random.uniform(ks[6], (d,), jnp.float32, -s, s)
        beta = jnp.ones((len(NUM_SCALES),), dtype=jnp.float32)
        return {'x': x, 'Wq': Wq, 'bq': bq, 'Wk': Wk, 'bk': bk, 'Wv': Wv, 'bv': bv, 'beta': beta}
    _L0_attn_all = _L0_attn_setup()
    _L0_attn_in = {k: v for k, v in _L0_attn_all.items() if k in ('Wq', 'bq', 'Wk', 'bk', 'Wv', 'bv', 'beta')}
    del _L0_attn_all

    def _L0_ffn_setup():
        import jax, jax.numpy as jnp
        import numpy as np
        B, K, D = (128, 16, 64)
        E = 32
        H = int(D * 0.25)
        key = jax.random.key(seed)
        ks = jax.random.split(key, 7)
        d_rs = D ** (-0.5)
        h_rs = H ** (-0.5)
        x = jax.random.normal(ks[0], (B, K, D), dtype=jnp.float32)
        router_w = jax.random.uniform(ks[1], (E, D), jnp.float32, -d_rs, d_rs)
        router_b = jax.random.uniform(ks[2], (E,), jnp.float32, -d_rs, d_rs)
        W1 = jax.random.uniform(ks[3], (E, D, H), jnp.float32, -h_rs, h_rs)
        b1 = jax.random.uniform(ks[4], (E, H), jnp.float32, -h_rs, h_rs)
        W2 = jax.random.uniform(ks[5], (E, H, D), jnp.float32, -d_rs, d_rs)
        b2 = jax.random.uniform(ks[6], (E, D), jnp.float32, -d_rs, d_rs)
        return {'x': x, 'router_w': router_w, 'router_b': router_b, 'W1': W1, 'b1': b1, 'W2': W2, 'b2': b2}
    _L0_ffn_all = _L0_ffn_setup()
    _L0_ffn_in = {k: v for k, v in _L0_ffn_all.items() if k in ('router_w', 'router_b', 'W1', 'b1', 'W2', 'b2')}
    del _L0_ffn_all
    return {'x': x, 'L0_tok_W': _L0_tok_in['W'], 'L0_attn_Wq': _L0_attn_in['Wq'], 'L0_attn_bq': _L0_attn_in['bq'], 'L0_attn_Wk': _L0_attn_in['Wk'], 'L0_attn_bk': _L0_attn_in['bk'], 'L0_attn_Wv': _L0_attn_in['Wv'], 'L0_attn_bv': _L0_attn_in['bv'], 'L0_attn_beta': _L0_attn_in['beta'], 'L0_ffn_router_w': _L0_ffn_in['router_w'], 'L0_ffn_router_b': _L0_ffn_in['router_b'], 'L0_ffn_W1': _L0_ffn_in['W1'], 'L0_ffn_b1': _L0_ffn_in['b1'], 'L0_ffn_W2': _L0_ffn_in['W2'], 'L0_ffn_b2': _L0_ffn_in['b2']}

def reference(x, L0_tok_W, L0_attn_Wq, L0_attn_bq, L0_attn_Wk, L0_attn_bk, L0_attn_Wv, L0_attn_bv, L0_attn_beta, L0_ffn_router_w, L0_ffn_router_b, L0_ffn_W1, L0_ffn_b1, L0_ffn_W2, L0_ffn_b2):
    import jax
    import jax.numpy as jnp

    def _L0_tok_ref(x, W):
        import jax, jax.numpy as jnp
        import numpy as np
        VOCAB = 50257
        DIM = 64

        def _positional_table(seq_len, dim, dtype=jnp.float32):
            pos = jnp.arange(seq_len, dtype=dtype)[:, None]
            d = jnp.arange(dim)
            exponent = (d - d % 2).astype(dtype) / dim
            inv_freq = jnp.power(jnp.asarray(10000.0, dtype), -exponent)
            angle = pos * inv_freq
            return jnp.where(d % 2 == 0, jnp.sin(angle), jnp.cos(angle))
        seq_len = x.shape[1]
        pe = _positional_table(seq_len, W.shape[1], W.dtype)
        return W[x] + pe[None, :, :]

    def _L0_attn_ref(x, Wq, bq, Wk, bk, Wv, bv, beta):
        import jax, jax.numpy as jnp
        import numpy as np
        import math
        EMBED_DIM = 64
        SEQ_LEN = 1024
        BATCH = 4
        NUM_SCALES = (24.0, 720.0)
        d = x.shape[-1]
        seq_len = x.shape[1]
        sqrt_d = jnp.asarray(math.sqrt(d), x.dtype)
        Q = jnp.einsum('bsd,ed->bse', x, Wq) + bq
        K = jnp.einsum('bsd,ed->bse', x, Wk) + bk
        V = jnp.einsum('bsd,ed->bse', x, Wv) + bv
        attn = jnp.einsum('bse,bte->bst', Q, K) / sqrt_d
        idx = jnp.arange(seq_len, dtype=jnp.float32)
        absdiff = jnp.abs(idx[:, None] - idx[None, :])
        two_pi = jnp.asarray(2.0 * math.pi, jnp.float32)
        bias = jnp.zeros((seq_len, seq_len), dtype=jnp.float32)
        for n, T in enumerate(NUM_SCALES):
            bias = bias + beta[n] * jnp.cos(two_pi * absdiff / T)
        scores = jax.nn.softmax(attn + bias[None, :, :], axis=-1)
        return jnp.einsum('bst,bte->bse', scores, V)

    def _L0_ffn_ref(x, router_w, router_b, W1, b1, W2, b2):
        import jax, jax.numpy as jnp
        import numpy as np
        B, K, D = (128, 16, 64)
        E = 32
        H = int(D * 0.25)
        xf = x.reshape(-1, D)
        logits = xf @ router_w.T + router_b
        idx = jnp.argmax(logits, axis=-1)
        w1t = jnp.take(W1, idx, axis=0)
        h = jnp.einsum('nd,ndh->nh', xf, w1t) + jnp.take(b1, idx, axis=0)
        h = jax.nn.relu(h)
        w2t = jnp.take(W2, idx, axis=0)
        out = jnp.einsum('nh,nhd->nd', h, w2t) + jnp.take(b2, idx, axis=0)
        out = jax.nn.relu(out)
        return out.reshape(x.shape)
    h = _L0_tok_ref(x, L0_tok_W)
    h = h + _L0_attn_ref(_layernorm(h, axis=-1), L0_attn_Wq, L0_attn_bq, L0_attn_Wk, L0_attn_bk, L0_attn_Wv, L0_attn_bv, L0_attn_beta)
    h = h + _L0_ffn_ref(_layernorm(h, axis=-1), L0_ffn_router_w, L0_ffn_router_b, L0_ffn_W1, L0_ffn_b1, L0_ffn_W2, L0_ffn_b2)
    return h

_drawn_inputs = setup_inputs


def setup_inputs(seed=0):
    import zlib

    import numpy as np

    out = dict(_drawn_inputs(seed))
    spreads = {'L0_attn_beta': (1.0, 0.6)}
    factors = {'L0_attn_bq': 6.221, 'L0_attn_bk': 8.0, 'L0_ffn_b1': 3.732}
    for name, (base, spread) in spreads.items():
        noise = np.random.default_rng([zlib.crc32(name.encode()), seed]).standard_normal(out[name].shape)
        drawn = base * np.exp(spread * noise) if base else spread * noise
        out[name] = jnp.asarray(drawn.astype(out[name].dtype))
    for name, factor in factors.items():
        out[name] = (out[name] * factor).astype(out[name].dtype)
    return out
```

```python
from contextlib import ExitStack

import numpy as np

import concourse.bass as bass
from concourse import mybir

ALU = mybir.AluOpType
ACT = mybir.ActivationFunctionType
F32 = mybir.dt.float32
F32R = mybir.dt.float32r
BF16 = mybir.dt.bfloat16
I32 = mybir.dt.int32
AX = mybir.AxisListType

P = 128
S, D = 2048, 64
NT = S // P
CH = 4
NC = NT // CH
E, H = 32, 16
NB = E * H // P
EPS = 1e-5
SCALES = (24.0, 720.0)
BIG = 2.0 ** 100
RSQRT_MAGIC = 1597463007.0
GROUPS = [(0, 4), (4, 4), (8, 4), (12, 4)]
STAGE_AT = [0, 2, 5, 7, 8, 9, 10, 12]
XN_SLOTS = 4


def tables():
    d = np.arange(D)
    inv = np.power(10000.0, -((d - d % 2) / D)).astype(np.float32)
    angle = (np.arange(S, dtype=np.float32)[:, None] * inv).astype(np.float64)
    pos = np.where(d % 2 == 0, np.sin(angle), np.cos(angle)).astype(np.float32)
    w = 2.0 * np.pi / np.array(SCALES)[:, None]
    row = w * (NT * np.arange(P))[None, :]
    col = w * (NT * np.arange(P)[None, :] + np.arange(1 - NT, NT)[:, None]).reshape(1, -1)
    by_row = np.concatenate([np.cos(row), np.sin(row)]).astype(np.float32)
    by_col = np.concatenate([np.cos(col), np.sin(col)]).astype(np.float32)
    ident = np.eye(P, dtype=np.float32)
    rev = np.broadcast_to((E - np.arange(E)).astype(np.float32), (P, E))
    mask = np.where(np.arange(E)[:, None] == np.arange(E * H)[None, :] // H, BIG, 0.0).astype(np.float32)
    return {
        "c_pos": pos.reshape(P, NT * D),
        "c_row": by_row,
        "c_col": by_col,
        "c_ident": np.concatenate([ident, rev], axis=1),
        "c_mask": mask,
    }


def build(nc, x, tok_w, wq, bq, wk, bk, wv, bv, beta, rw, rb, w1, b1, w2, b2,
          c_pos, c_row, c_col, c_ident, c_mask, out):
    GW = (2 * NT - 1) * P
    last_slot = 4 * NT + 1

    stages = {}
    for g, (t0, n) in enumerate(GROUPS):
        base = 4 * (t0 + n) + 1 + XN_SLOTS
        for j, at in enumerate(STAGE_AT):
            stages.setdefault(base + at, []).append((g, j))
    end_slot = max(stages) + 1
    group_end = {t0 + n - 1: g for g, (t0, n) in enumerate(GROUPS)}
    slots = range(-8, end_slot)

    with ExitStack() as ctx:
        def sb(name, shape, dt=F32):
            return ctx.enter_context(nc.sbuf_tensor(name, shape, dt))

        def ps(name, shape):
            return ctx.enter_context(nc.psum_tensor(name, shape, F32))

        def sem(name):
            return ctx.enter_context(nc.semaphore(name))

        idx = sb("idx", [P, NT], I32)
        pos = sb("pos", [P, NT, D])
        ident_rev = sb("ident_rev", [P, P + E])
        ident, rev = ident_rev[:, 0:P], ident_rev[:, P:P + E]
        by_row = sb("by_row", [4, P])
        by_row_beta = sb("by_row_beta", [4, P])
        by_col = sb("by_col", [4, GW])
        beta_col = sb("beta_col", [4, 1])
        bias = sb("bias", [P, GW])
        h0 = sb("h0", [P, NT, D])
        stats1 = sb("stats1", [P, NT, 6])
        mv1 = sb("mv1", [P, NT, 2])
        rs = sb("rs", [P, 6, NT])
        rstd1 = sb("rstd1", [P, NT])
        xn1 = sb("xn1", [P, NT, D])
        xt = sb("xt", [D + 1, S])
        w_nat = sb("w_nat", [D, 3 * D])
        w_qt = sb("w_qt", [D + 1, 2 * D])
        w_kt = sb("w_kt", [D + 1, 2 * D])
        w_vt = sb("w_vt", [D + 1, D])
        q_split = sb("q_split", [P, S], F32R)
        k_hi = sb("k_hi", [P, S], F32R)
        k_lo = sb("k_lo", [P, S], F32R)
        v = sb("v", [P, NT, D])
        sc = sb("sc", [P, 2, S])
        pmax = sb("pmax", [P, NT, 2])
        nmax = sb("nmax", [P, NT])
        pr = sb("pr", [P, 2, S])
        psumh = sb("psumh", [P, NT, 2])
        den = sb("den", [P, NT])
        rden = sb("rden", [P, NT])
        prt = sb("prt", [P, 4, 512])
        h1 = sb("h1", [P, NT, D])
        stats2 = sb("stats2", [P, NT, 6])
        mv2 = sb("mv2", [P, NT, 2])
        rstd2 = sb("rstd2", [P, NT])
        xn2 = sb("xn2", [P, CH, D])
        xn2_split = sb("xn2_split", [P, CH, 2 * D], F32R)
        x2t = sb("x2t", [P, CH * P], F32R)
        rw_nat = sb("rw_nat", [E, 2 * D])
        rw_t = sb("rw_t", [P, E])
        rw_hi = sb("rw_hi", [P, E], F32R)
        rw_lo = sb("rw_lo", [P, E], F32R)
        rb_all = sb("rb_all", [P, E])
        logit = sb("logit", [P, CH, E])
        lmax = sb("lmax", [P, CH])
        tie = sb("tie", [P, CH, E])
        tmax = sb("tmax", [P, CH])
        chosen = sb("chosen", [P, CH, E])
        chosen_t = sb("chosen_t", [E, CH * P])
        unchosen_t = sb("unchosen_t", [E, CH * P], BF16)
        mask_f = sb("mask_f", [E, E * H])
        mask = sb("mask", [E, E * H], BF16)
        w1_nat = sb("w1_nat", [P, E, H])
        w1_hi = sb("w1_hi", [P, E * H], F32R)
        w1_lo = sb("w1_lo", [P, E * H], F32R)
        b1_nat = sb("b1_nat", [NB, P])
        b1_col = sb("b1_col", [P, NB])
        w2_s = sb("w2_s", [P, NB, D])
        b2_s = sb("b2_s", [E, D])
        hid = sb("hid", [P, NB, CH * P])
        res = sb("res", [P, NT, D])

        ps_s = ps("ps_s", [P, S])
        ps_t = ps("ps_t", [P, 2, 512])
        ps_o = ps("ps_o", [P, 512])
        ps_f = ps("ps_f", [P, 512])

        idx_in, pos_in, const_in = sem("idx_in"), sem("pos_in"), sem("const_in")
        biasf_in, wqkv_in, wexp_in = sem("biasf_in"), sem("wqkv_in"), sem("wexp_in")
        tok_in = [sem(f"tok_in{c}") for c in range(NC)]
        out_sent = sem("out_sent")
        row_ready, biasmm, bias_act, bias_dve = sem("row_ready"), sem("biasmm"), sem("bias_act"), sem("bias_dve")
        wt_turned, wt_ready = sem("wt_turned"), sem("wt_ready")
        ones_set = sem("ones_set")
        xn1_ready, xt_turned, xt_ready = sem("xn1_ready"), sem("xt_turned"), sem("xt_ready")
        q_mm, k_mm, v_mm = sem("q_mm"), sem("k_mm"), sem("v_mm")
        q_hi_done, k_hi_done, q_ready, k_ready, v_ready = (
            sem("q_hi_done"), sem("k_hi_done"), sem("q_ready"), sem("k_ready"), sem("v_ready"))
        expw_ready = sem("expw_ready")
        s_mm = sem("s_mm")
        s_read = sem("s_read")
        nmax_ready = sem("nmax_ready")
        exp_done = sem("exp_done")
        p_turned = sem("p_turned")
        prt_act, prt_dve = sem("prt_act"), sem("prt_dve")
        pv_mm = sem("pv_mm")
        h1_done = sem("h1_done")
        rstd2_ready, xs_ready = sem("rstd2_ready"), sem("xs_ready")
        x2_turned, x2t_ready = sem("x2_turned"), sem("x2t_ready")
        logit_mm, chosen_ready, chosen_turned = sem("logit_mm"), sem("chosen_ready"), sem("chosen_turned")
        chosen_t_ready, unchosen_t_ready = sem("chosen_t_ready"), sem("unchosen_t_ready")
        hid_mm, hid_ready, out_mm, res_done = sem("hid_mm"), sem("hid_ready"), sem("out_mm"), sem("res_done")
        logit_read = sem("logit_read")
        dve_step, pool_step, act_step = sem("dve_step"), sem("pool_step"), sem("act_step")

        block = ctx.enter_context(nc.Block())

        BW = [min(512, GW - 512 * j) for j in range(-(-GW // 512))]
        half = S // 2

        def prt_by_act(k):
            return k % 4 != 1

        def prt_count(k):
            return sum(prt_by_act(j) == prt_by_act(k) for j in range(k + 1))

        def wait_prt(eng, k):
            eng.wait_ge(prt_act if prt_by_act(k) else prt_dve, prt_count(k))

        @block.sync
        def _(sp):
            sp.dma_start(idx[:, :], x.rearrange("a (p i) -> (a p) i", p=P)).then_inc(idx_in, 16)
            sp.dma_start(by_row[:, :], c_row).then_inc(biasf_in, 16)
            sp.dma_start(beta_col[0:2, :], beta.rearrange("(b o) -> b o", o=1)).then_inc(biasf_in, 16)
            sp.dma_start(beta_col[2:4, :], beta.rearrange("(b o) -> b o", o=1)).then_inc(biasf_in, 16)
            sp.dma_start(by_col[:, :], c_col).then_inc(biasf_in, 16)
            sp.dma_start(pos[:, :, :], c_pos.rearrange("p (i d) -> p i d", d=D)).then_inc(pos_in, 16)
            w1_v = w1.rearrange("e d h -> d e h")
            sp.dma_start(w1_nat[0:D, :, :], w1_v).then_inc(wexp_in, 16)
            sp.dma_start(w1_nat[D:2 * D, :, :], w1_v).then_inc(wexp_in, 16)
            sp.dma_start(mask_f[:, :], c_mask).then_inc(wexp_in, 16)
            sp.dma_start(w2_s[:, :, :], w2.rearrange("(b e) h d -> (e h) b d", b=NB)).then_inc(wexp_in, 16)
            sp.dma_start(b2_s[:, :], b2).then_inc(wexp_in, 16)
            sp.dma_start(rb_all[:, :], rb.partition_broadcast(P)).then_inc(wexp_in, 16)
            out_v = out.rearrange("a (p i) d -> (a p) i d", p=P)
            for g, (t0, n) in enumerate(GROUPS):
                sp.wait_ge(res_done, g + 1)
                sp.dma_start(out_v[:, t0:t0 + n, :], res[:, t0:t0 + n, :]).then_inc(out_sent, 16)
            sp.wait_ge(out_sent, 16 * len(GROUPS))

        @block.gpsimd
        def _(pool):
            pool.wait_ge(idx_in, 16)
            for i in range(NT):
                nc.gpsimd.indirect_dma_start(
                    out=h0[:, i, :], out_offset=None, in_=tok_w,
                    in_offset=bass.IndirectOffsetOnAxis(ap=idx[:, i:i + 1], axis=0),
                ).then_inc(tok_in[i // CH], 16)
            steps = 0
            for g, (t0, n) in enumerate(GROUPS):
                pool.wait_ge(rstd2_ready, g + 1)
                if g >= 1:
                    pool.wait_ge(x2_turned, g)
                for t in range(n):
                    nc.gpsimd.tensor_scalar(xn2[:, t, :], h1[:, t0 + t, :], mv2[:, t0 + t, 0:1],
                                            rstd2[:, t0 + t:t0 + t + 1], ALU.subtract, ALU.mult).then_inc(pool_step, 1)
                steps += n
                pool.wait_ge(pool_step, steps)
                nc.gpsimd.tensor_copy(xn2_split[:, 0:n, 0:D], xn2[:, 0:n, :]).then_inc(pool_step, 1)
                steps += 1
                pool.wait_ge(pool_step, steps)
                nc.gpsimd.tensor_tensor(xn2_split[:, 0:n, D:2 * D], xn2[:, 0:n, :],
                                        xn2_split[:, 0:n, 0:D].bitcast(F32), ALU.subtract).then_inc(xs_ready, 1)

        @block.scalar
        def _(act):
            act.dma_start(ident_rev[:, :], c_ident).then_inc(const_in, 16)
            act.dma_start(w_nat[:, 0:D], wq).then_inc(wqkv_in, 16)
            act.dma_start(w_nat[:, D:2 * D], wk).then_inc(wqkv_in, 16)
            act.dma_start(w_nat[:, 2 * D:3 * D], wv).then_inc(wqkv_in, 16)
            act.dma_start(b1_nat[:, :], b1.rearrange("(b e) h -> b (e h)", b=NB)).then_inc(wqkv_in, 16)
            act.dma_start(rw_nat[:, 0:D], rw).then_inc(wqkv_in, 16)
            act.dma_start(rw_nat[:, D:2 * D], rw).then_inc(wqkv_in, 16)
            for w, b in ((w_qt, bq), (w_kt, bk)):
                for r in range(2):
                    act.dma_start(w[D:D + 1, r * D:(r + 1) * D], b.rearrange("(a d) -> a d", a=1)).then_inc(wqkv_in, 16)
            act.dma_start(w_vt[D:D + 1, :], bv.rearrange("(a d) -> a d", a=1)).then_inc(wqkv_in, 16)
            for j in range(1, len(BW), 2):
                act.wait_ge(biasmm, j + 1)
                nc.scalar.activation(bias[:, 512 * j:512 * j + BW[j]], ps_s[:, 512 * (j % 4):512 * (j % 4) + BW[j]],
                                     ACT.Copy).then_inc(bias_act, 1)
            for c in range(NC):
                cols = slice(c * 512, (c + 1) * 512)
                act.wait_ge(xt_turned, c + 1)
                nc.scalar.activation(xt[0:D, cols], ps_t[0:D, c % 2, :], ACT.Copy).then_inc(xt_ready, 1)
                act.wait_ge(q_mm, c + 1)
                nc.scalar.activation(q_split[:, cols], ps_o[:, :], ACT.Copy, scale=D ** -0.5).then_inc(q_hi_done, 1)
                act.wait_ge(k_mm, c + 1)
                nc.scalar.activation(k_hi[:, cols], ps_f[:, :], ACT.Copy).then_inc(k_hi_done, 1)
                act.wait_ge(v_mm, c + 1)
                nc.scalar.activation(v[:, CH * c:CH * (c + 1), :], ps_s[:, 512 * c:512 * c + CH * D],
                                     ACT.Copy).then_inc(v_ready, 1)

            def exp_half(i, a):
                if i < 0 or i >= NT:
                    return
                if a == 0:
                    act.wait_ge(nmax_ready, i + 1)
                if i >= 2:
                    act.wait_ge(p_turned, 4 * (i - 2) + 2 * (a + 1))
                cols = slice(a * half, (a + 1) * half)
                nc.scalar.activation(pr[:, i % 2, cols], sc[:, i % 2, cols], ACT.Exp, bias=nmax[:, i:i + 1],
                                     accum_out=psumh[:, i, a:a + 1]).then_inc(exp_done, 1)

            def copy_prt(k):
                act.wait_ge(p_turned, k + 1)
                if k >= 4:
                    act.wait_ge(pv_mm, k - 3)
                nc.scalar.activation(prt[:, k % 4, :], ps_t[:, k % 2, :], ACT.Copy).then_inc(prt_act, 1)

            def expert(g, j):
                t0, n = GROUPS[g]
                w = n * P
                if j == 0:
                    act.wait_ge(x2_turned, g + 1)
                    nc.scalar.activation(x2t[:, 0:w], ps_f[:, 0:w], ACT.Copy).then_inc(x2t_ready, 1)
                elif j == 2:
                    act.wait_ge(chosen_turned, g + 1)
                    nc.scalar.activation(chosen_t[:, 0:w], ps_f[0:E, 0:w], ACT.Copy).then_inc(chosen_t_ready, 1)
                elif 3 <= j <= 6:
                    b = j - 3
                    act.wait_ge(hid_mm, NB * g + b + 1)
                    if b == 0 and g >= 1:
                        act.wait_ge(out_mm, g)
                    if b == 0 and g == 0:
                        act.wait_ge(wt_ready, 1)
                    nc.scalar.activation(hid[:, b, 0:w], ps_f[:, 0:w], ACT.Relu, bias=b1_col[:, b:b + 1]
                                         ).then_inc(hid_ready, 1)

            for k in slots:
                i, q = k // 4, k % 4
                if 0 <= k < 4 * NT and prt_by_act(k):
                    copy_prt(k)
                if q == 1:
                    exp_half(i + 1, 0)
                if q == 2:
                    exp_half(i + 1, 1)
                for g, j in stages.get(k, []):
                    expert(g, j)

        @block.tensor
        def _(pe):
            pe.wait_ge(const_in, 16)
            pe.wait_ge(wqkv_in, 11 * 16)
            for r in range(3):
                nc.tensor.transpose(ps_t[0:D, 0, r * D:(r + 1) * D], w_nat[:, r * D:(r + 1) * D], ident[0:D, 0:D])
            nc.tensor.transpose(ps_t[:, 0, 3 * D + E:3 * D + E + NB], b1_nat[:, :], ident[0:NB, 0:NB])
            nc.tensor.transpose(ps_t[:, 0, 3 * D:3 * D + E], rw_nat[:, :], ident[0:E, 0:E]).then_inc(wt_turned, 1)
            pe.wait_ge(row_ready, 1)
            for j, w in enumerate(BW):
                if j >= 4:
                    pe.wait_ge(*((bias_act, (j - 4) // 2 + 1) if j % 2 else (bias_dve, (j - 4) // 2 + 1)))
                nc.tensor.matmul(ps_s[:, 512 * (j % 4):512 * (j % 4) + w], by_row_beta[:, :],
                                 by_col[:, 512 * j:512 * j + w], start=True, stop=True).then_inc(biasmm, 1)
            for c in range(NC):
                cols = slice(c * 512, (c + 1) * 512)
                pe.wait_ge(xn1_ready, c + 1)
                if c == 0:
                    pe.wait_ge(wt_ready, 1)
                if c >= 2:
                    pe.wait_ge(xt_ready, c - 1)
                for t in range(CH):
                    mm = nc.tensor.transpose(ps_t[0:D, c % 2, t * P:(t + 1) * P], xn1[:, CH * c + t, :], ident)
                mm.then_inc(xt_turned, 1)
                pe.wait_ge(xt_ready, c + 1)
                if c == 0:
                    pe.wait_ge(ones_set, 1)
                else:
                    pe.wait_ge(q_ready, c)
                nc.tensor.matmul(ps_o[:, :], w_qt[:, :], xt[:, cols], start=True, stop=True).then_inc(q_mm, 1)
                if c >= 1:
                    pe.wait_ge(k_ready, c)
                nc.tensor.matmul(ps_f[:, :], w_kt[:, :], xt[:, cols], start=True, stop=True).then_inc(k_mm, 1)
                if c == 0:
                    pe.wait_ge(bias_act, len(BW) // 2)
                    pe.wait_ge(bias_dve, (len(BW) + 1) // 2)
                for t in range(CH):
                    mm = nc.tensor.matmul(ps_s[:, 512 * c + t * D:512 * c + (t + 1) * D],
                                          xt[:, (CH * c + t) * P:(CH * c + t + 1) * P], w_vt[:, :],
                                          start=True, stop=True)
                mm.then_inc(v_mm, 1)

            def scores(i, b):
                if i >= NT:
                    return
                if i == 0 and b == 0:
                    pe.wait_ge(q_ready, NC)
                    pe.wait_ge(k_ready, NC)
                    pe.wait_ge(v_ready, NC)
                if i >= 1 and b % 2 == 0:
                    pe.wait_ge(s_read, 2 * (i - 1) + b // 2 + 1)
                queries = q_split[:, i * P:(i + 1) * P]
                keys = slice(b * 512, (b + 1) * 512)
                nc.tensor.matmul(ps_s[:, keys], queries, k_hi[:, keys], start=True, stop=False)
                mm = nc.tensor.matmul(ps_s[:, keys], queries, k_lo[:, keys], start=False, stop=True)
                if b % 2:
                    mm.then_inc(s_mm, 1)

            def turn(k):
                i, q = k // 4, k % 4
                if q % 2 == 0:
                    pe.wait_ge(exp_done, 2 * i + q // 2 + 1)
                if k >= 2:
                    wait_prt(pe, k - 2)
                for t in range(4):
                    mm = nc.tensor.transpose(ps_t[:, k % 2, t * P:(t + 1) * P],
                                             pr[:, i % 2, (4 * q + t) * P:(4 * q + t + 1) * P], ident)
                mm.then_inc(p_turned, 1)

            def times_v(k):
                i, q = k // 4, k % 4
                wait_prt(pe, k)
                if q == 0 and i >= 1:
                    pe.wait_ge(h1_done, i)
                for t in range(4):
                    mm = nc.tensor.matmul(ps_o[:, 0:D], prt[:, k % 4, t * P:(t + 1) * P], v[:, 4 * q + t, :],
                                          start=(q == 0 and t == 0), stop=(q == 3 and t == 3))
                mm.then_inc(pv_mm, 1)

            def expert(g, j):
                t0, n = GROUPS[g]
                w = n * P
                if j == 0:
                    pe.wait_ge(xs_ready, g + 1)
                    if g >= 1:
                        pe.wait_ge(res_done, g)
                    for t in range(n):
                        mm = nc.tensor.transpose(ps_f[:, t * P:(t + 1) * P], xn2_split[:, t, :].bitcast(F32), ident)
                    mm.then_inc(x2_turned, 1)
                elif j == 1:
                    pe.wait_ge(x2t_ready, g + 1)
                    pe.wait_ge(expw_ready, 1)
                    for t in range(n):
                        x_t = x2t[:, t * P:(t + 1) * P]
                        nc.tensor.matmul(ps_f[:, t * E:(t + 1) * E], x_t, rw_hi[:, :], start=True, stop=False)
                        mm = nc.tensor.matmul(ps_f[:, t * E:(t + 1) * E], x_t, rw_lo[:, :], start=False, stop=True)
                    mm.then_inc(logit_mm, 1)
                elif j == 2:
                    pe.wait_ge(chosen_ready, g + 1)
                    for t in range(n):
                        mm = nc.tensor.transpose(ps_f[0:E, t * P:(t + 1) * P], chosen[:, t, :], ident)
                    mm.then_inc(chosen_turned, 1)
                elif j <= 6:
                    b = j - 3
                    if b == 0:
                        pe.wait_ge(chosen_t_ready, g + 1)
                        pe.wait_ge(unchosen_t_ready, g + 1)
                    else:
                        pe.wait_ge(hid_ready, NB * g + b)
                    rows = slice(b * P, (b + 1) * P)
                    nc.tensor.matmul(ps_f[:, 0:w], w1_hi[:, rows], x2t[:, 0:w], start=True, stop=False)
                    nc.tensor.matmul(ps_f[:, 0:w], w1_lo[:, rows], x2t[:, 0:w], start=False, stop=False)
                    nc.tensor.matmul(ps_f[:, 0:w], mask[:, rows], unchosen_t[:, 0:w],
                                     start=False, stop=True).then_inc(hid_mm, 1)
                else:
                    pe.wait_ge(hid_ready, NB * (g + 1))
                    for t in range(n):
                        toks = slice(t * P, (t + 1) * P)
                        o = ps_f[:, t * D:(t + 1) * D]
                        nc.tensor.matmul(o, chosen_t[:, toks], b2_s[:, :], start=True, stop=False)
                        for b in range(NB):
                            mm = nc.tensor.matmul(o, hid[:, b, toks], w2_s[:, b, :], start=False, stop=(b == NB - 1))
                    mm.then_inc(out_mm, 1)

            for k in slots:
                i, q = k // 4, k % 4
                if 2 <= k < 4 * NT + 2:
                    times_v(k - 2)
                if 0 <= k < 4 * NT:
                    turn(k)
                scores(i + 2, q)
                for g, j in stages.get(k, []):
                    expert(g, j)

        @block.vector
        def _(dve):
            steps = [0]

            def then_own(ins):
                ins.then_inc(dve_step, 1)
                steps[0] += 1
                dve.wait_ge(dve_step, steps[0])

            def rsqrt(dst, var, n):
                vv, y, t, u = (rs[:, r, 0:n] for r in range(4))
                then_own(nc.vector.tensor_scalar(vv, var, EPS, None, ALU.add))
                nc.vector.tensor_scalar(rs[:, 4, 0:n], vv, -0.5, None, ALU.mult)
                then_own(nc.vector.tensor_scalar(y.bitcast(I32), vv.bitcast(I32), -0.5, RSQRT_MAGIC, ALU.mult, ALU.add))
                for r in range(3):
                    then_own(nc.vector.tensor_tensor(t, y, y, ALU.mult))
                    then_own(nc.vector.tensor_tensor(u, t, rs[:, 4, 0:n], ALU.mult))
                    if r < 2:
                        then_own(nc.vector.scalar_tensor_tensor(y, u, 1.5, y, ALU.add, ALU.mult))
                return nc.vector.scalar_tensor_tensor(dst, u, 1.5, y, ALU.add, ALU.mult)

            nc.vector.memset(xt[D:D + 1, :], 1.0).then_inc(ones_set, 1)
            dve.wait_ge(biasf_in, 4 * 16)
            nc.vector.tensor_scalar(by_row_beta[:, :], by_row[:, :], beta_col[:, 0:1], None, ALU.mult).then_inc(row_ready, 1)
            dve.wait_ge(wt_turned, 1)
            for r, w in enumerate((w_qt, w_kt)):
                for s in range(2):
                    nc.vector.tensor_copy(w[0:D, s * D:(s + 1) * D], ps_t[0:D, 0, r * D:(r + 1) * D])
            nc.vector.tensor_copy(w_vt[0:D, :], ps_t[0:D, 0, 2 * D:3 * D])
            nc.vector.tensor_copy(b1_col[:, :], ps_t[:, 0, 3 * D + E:3 * D + E + NB])
            nc.vector.tensor_copy(rw_t[:, :], ps_t[:, 0, 3 * D:3 * D + E]).then_inc(wt_ready, 1)
            for j in range(0, len(BW), 2):
                dve.wait_ge(biasmm, j + 1)
                nc.vector.tensor_copy(bias[:, 512 * j:512 * j + BW[j]], ps_s[:, 512 * (j % 4):512 * (j % 4) + BW[j]]
                                      ).then_inc(bias_dve, 1)
            dve.wait_ge(wexp_in, 6 * 16)
            w1_f = w1_nat[:, :, :].rearrange("p e h -> p (e h)")
            nc.vector.tensor_copy(w1_hi[:, :], w1_f)
            nc.vector.tensor_copy(mask[:, :], mask_f[:, :])
            then_own(nc.vector.tensor_copy(rw_hi[:, :], rw_t[:, :]))
            nc.vector.tensor_tensor(w1_lo[:, :], w1_f, w1_hi[:, :].bitcast(F32), ALU.subtract)
            nc.vector.tensor_tensor(rw_lo[:, :], rw_t[:, :], rw_hi[:, :].bitcast(F32), ALU.subtract).then_inc(expw_ready, 1)

            dve.wait_ge(pos_in, 16)
            for c in range(NC):
                tiles = slice(CH * c, CH * (c + 1))
                cols = slice(c * 512, (c + 1) * 512)
                dve.wait_ge(tok_in[c], CH * 16)
                then_own(nc.vector.tensor_tensor(h0[:, tiles, :], h0[:, tiles, :], pos[:, tiles, :], ALU.add))
                for t in range(CH * c, CH * (c + 1)):
                    st = nc.vector.bn_stats(stats1[:, t, :], h0[:, t, :])
                then_own(st)
                for t in range(CH * c, CH * (c + 1)):
                    st = nc.vector.bn_aggr(mv1[:, t, :], stats1[:, t, :])
                then_own(st)
                then_own(rsqrt(rstd1[:, tiles], mv1[:, tiles, 1], CH))
                for t in range(CH * c, CH * (c + 1)):
                    st = nc.vector.tensor_scalar(xn1[:, t, :], h0[:, t, :], mv1[:, t, 0:1], rstd1[:, t:t + 1],
                                                 ALU.subtract, ALU.mult)
                st.then_inc(xn1_ready, 1)
                dve.wait_ge(q_hi_done, c + 1)
                nc.vector.scalar_tensor_tensor(q_split[D:2 * D, cols], ps_o[D:2 * D, :], D ** -0.5,
                                               q_split[D:2 * D, cols].bitcast(F32), ALU.mult, ALU.subtract
                                               ).then_inc(q_ready, 1)
                dve.wait_ge(k_hi_done, c + 1)
                nc.vector.tensor_tensor(k_lo[:, cols], ps_f[:, :], k_hi[:, cols].bitcast(F32), ALU.subtract
                                        ).then_inc(k_ready, 1)

            def add_bias(i, a):
                if i < 0 or i >= NT:
                    return
                dve.wait_ge(s_mm, 2 * i + a + 1)
                if i >= 2:
                    dve.wait_ge(exp_done, 2 * (i - 2) + a + 1)
                cols = slice(a * half, (a + 1) * half)
                b0 = (NT - 1 - i) * P + a * half
                nc.vector.tensor_tensor_reduce(sc[:, i % 2, cols], ps_s[:, cols], bias[:, b0:b0 + half], 1.0,
                                               -3.0e38, ALU.add, ALU.max, pmax[:, i, a:a + 1]).then_inc(s_read, 1)
                if a == 1:
                    dve.wait_ge(s_read, 2 * i + 2)
                    nc.vector.tensor_scalar(nmax[:, i:i + 1], pmax[:, i, 0:1], pmax[:, i, 1:2], -1.0,
                                            ALU.max, ALU.mult).then_inc(nmax_ready, 1)

            def copy_prt(k):
                dve.wait_ge(p_turned, k + 1)
                if k >= 4:
                    dve.wait_ge(pv_mm, k - 3)
                nc.vector.tensor_copy(prt[:, k % 4, :], ps_t[:, k % 2, :]).then_inc(prt_dve, 1)

            def residual(i):
                dve.wait_ge(exp_done, 2 * i + 2)
                then_own(nc.vector.tensor_tensor(den[:, i:i + 1], psumh[:, i, 0:1], psumh[:, i, 1:2], ALU.add))
                then_own(nc.vector.reciprocal(rden[:, i:i + 1], den[:, i:i + 1]))
                dve.wait_ge(pv_mm, 4 * (i + 1))
                nc.vector.scalar_tensor_tensor(h1[:, i, :], ps_o[:, 0:D], rden[:, i:i + 1], h0[:, i, :],
                                               ALU.mult, ALU.add).then_inc(h1_done, 1)
                dve.wait_ge(h1_done, i + 1)
                then_own(nc.vector.bn_stats(stats2[:, i, :], h1[:, i, :]))
                then_own(nc.vector.bn_aggr(mv2[:, i, :], stats2[:, i, :]))
                if i in group_end:
                    t0, n = GROUPS[group_end[i]]
                    rsqrt(rstd2[:, t0:t0 + n], mv2[:, t0:t0 + n, 1], n).then_inc(rstd2_ready, 1)

            def expert(g, j):
                t0, n = GROUPS[g]
                w = n * P
                if j == 1:
                    dve.wait_ge(logit_mm, g + 1)
                    lg, ti, ch = logit[:, 0:n, :], tie[:, 0:n, :], chosen[:, 0:n, :]
                    then_own(nc.vector.tensor_tensor(lg, ps_f[:, 0:n * E].rearrange("p (t e) -> p t e", e=E),
                                                     rb_all[:, :].unsqueeze(1).to_broadcast([P, n, E]), ALU.add))
                    then_own(nc.vector.tensor_reduce(lmax[:, 0:n], lg, AX.X, ALU.max))
                    then_own(nc.vector.tensor_tensor(ti, lg, lmax[:, 0:n].unsqueeze(2).to_broadcast([P, n, E]),
                                                     ALU.is_equal))
                    then_own(nc.vector.tensor_tensor(ti, ti, rev.unsqueeze(1).to_broadcast([P, n, E]), ALU.mult))
                    then_own(nc.vector.tensor_reduce(tmax[:, 0:n], ti, AX.X, ALU.max))
                    nc.vector.tensor_tensor(ch, ti, tmax[:, 0:n].unsqueeze(2).to_broadcast([P, n, E]),
                                            ALU.is_equal).then_inc(chosen_ready, 1)
                elif j == 2:
                    dve.wait_ge(chosen_t_ready, g + 1)
                    nc.vector.tensor_scalar(unchosen_t[:, 0:w], chosen_t[:, 0:w], -1.0, None, ALU.add
                                            ).then_inc(unchosen_t_ready, 1)
                elif j == 7:
                    dve.wait_ge(out_mm, g + 1)
                    nc.vector.scalar_tensor_tensor(res[:, t0:t0 + n, :], ps_f[:, 0:n * D].rearrange("p (t d) -> p t d", d=D),
                                                   0.0, h1[:, t0:t0 + n, :], ALU.max, ALU.add).then_inc(res_done, 1)

            for k in slots:
                i, q = k // 4, k % 4
                if q == 1 and 0 <= i - 1 < NT:
                    residual(i - 1)
                if 0 <= k < 4 * NT and not prt_by_act(k):
                    copy_prt(k)
                if q == 2:
                    add_bias(i + 2, 0)
                if q == 0:
                    add_bias(i + 1, 1)
                for g, j in stages.get(k, []):
                    expert(g, j)


_INS = ["x", "L0_tok_W", "L0_attn_Wq", "L0_attn_bq", "L0_attn_Wk", "L0_attn_bk", "L0_attn_Wv", "L0_attn_bv",
        "L0_attn_beta", "L0_ffn_router_w", "L0_ffn_router_b", "L0_ffn_W1", "L0_ffn_b1", "L0_ffn_W2", "L0_ffn_b2"]


def kernel(**inputs):
    import numpy as _np
    import concourse.bacc as _bacc
    from concourse import mybir as _mybir
    from concourse.bass_utils import run_bass_kernel_spmd as _run

    nc = _bacc.Bacc("TRN2", target_bir_lowering=False, num_devices=1)
    arrays, args = {}, []
    host = {name: _np.ascontiguousarray(inputs[name]) for name in _INS}
    host.update({name: _np.ascontiguousarray(a) for name, a in tables().items()})
    for name, a in host.items():
        arrays[f"in_{name}"] = a
        args.append(nc.dram_tensor(f"in_{name}", a.shape, _mybir.dt.from_np(a.dtype), kind="ExternalInput").ap())
    args.append(nc.dram_tensor("out_0", (1, S, D), _mybir.dt.float32, kind="ExternalOutput").ap())
    build(nc, *args)
    r = _run(nc, [arrays], core_ids=[0])
    return r.results[0]["out_0"]
```

```python
from contextlib import ExitStack

import numpy as np

import concourse.bass as bass
from concourse import mybir

ALU = mybir.AluOpType
ACT = mybir.ActivationFunctionType
F32 = mybir.dt.float32
F32R = mybir.dt.float32r
BF16 = mybir.dt.bfloat16
I32 = mybir.dt.int32
AX = mybir.AxisListType

P = 128
S, D = 2048, 64
NT = S // P
CH = 4
NC = NT // CH
E, H = 32, 16
NB = E * H // P
EPS = 1e-5
SCALES = (24.0, 720.0)
BIG = 2.0 ** 100
RSQRT_MAGIC = 1597463007.0
GROUPS = [(0, 4), (4, 4), (8, 4), (12, 2), (14, 2)]
STAGE_SLOTS = [[31, 33, 40, 46, 48, 49, 51, 55, 57],
               [48, 50, 57, 58, 59, 60, 62, 65, 67],
               [63, 65, 71, 72, 73, 74, 75, 77, 78],
               [70, 71, 77, 81, 82, 83, 84, 85, 86],
               [76, 77, 84, 85, 89, 90, 91, 92, 93]]
EARLY = 3
LAG = 14
NB_S, NB_T, NB_F = 2, 3, 2
POOL_HIDDEN = (5, 6)
EXP_LAG = 6
OUT_LAG = 12
LAST_AT = 71


def tables():
    d = np.arange(D)
    inv = np.power(10000.0, -((d - d % 2) / D)).astype(np.float32)
    angle = (np.arange(S, dtype=np.float32)[:, None] * inv).astype(np.float64)
    pos = np.where(d % 2 == 0, np.sin(angle), np.cos(angle)).astype(np.float32)
    w = 2.0 * np.pi / np.array(SCALES)[:, None]
    row = w * (NT * np.arange(P))[None, :]
    col = w * (NT * np.arange(P)[None, :] + np.arange(1 - NT, NT)[:, None]).reshape(1, -1)
    by_row = np.concatenate([np.cos(row), np.sin(row)]).astype(np.float32)
    by_col = np.concatenate([np.cos(col), np.sin(col)]).astype(np.float32)
    ident = np.eye(P, dtype=np.float32)
    rev = np.broadcast_to((E - np.arange(E)).astype(np.float32), (P, E))
    mask = np.where(np.arange(E)[:, None] == np.arange(E * H)[None, :] // H, 0.0, -BIG).astype(np.float32)
    col_hi = ((by_col.view(np.uint32) + np.uint32(0x800)) & np.uint32(0xFFFFF000)).view(np.float32)
    is_lo = np.repeat([0.0, 1.0], 8)[:, None]
    is_scale = np.tile(np.eye(2), (8, 1))
    return {
        "c_pos": pos.reshape(P, NT * D),
        "c_row": np.concatenate([np.tile(by_row, (4, 1)), is_lo, is_scale], axis=1).astype(np.float32),
        "c_col": np.tile(np.concatenate([col_hi, by_col - col_hi]), (2, 1)).astype(np.float32),
        "c_ident": np.concatenate([ident, rev, ident[:, 0:D] + ident[:, D:P]], axis=1),
        "c_mask": mask,
    }


def build(nc, x, tok_w, wq, bq, wk, bk, wv, bv, beta, rw, rb, w1, b1, w2, b2,
          c_pos, c_row, c_col, c_ident, c_mask, out):
    GW = (2 * NT - 1) * P
    WQ, WK, WV, WR = (slice(0, 2 * D), slice(2 * D, 4 * D), slice(4 * D, 5 * D), slice(5 * D, 5 * D + E))
    WC = 5 * D + E

    stages = {}
    for g, slots_of in enumerate(STAGE_SLOTS):
        for j, at in enumerate(slots_of):
            stages.setdefault(at, []).append((g, j))
    end_slot = max(stages) + 1
    slots = range(-LAG, end_slot)
    group_of = {t // 2: g for g, (t0, n) in enumerate(GROUPS) for t in range(t0, t0 + n, 2)}
    late_q, late_v = {4 - LAG: 2, 6 - LAG: 3}, {5 - LAG: 2, 7 - LAG: 3}
    NPAIR = NT // 2
    TAIL = len(GROUPS) - 1

    with ExitStack() as ctx:
        def sb(name, shape, dt=F32):
            return ctx.enter_context(nc.sbuf_tensor(name, shape, dt))

        def ps(name, shape):
            return ctx.enter_context(nc.psum_tensor(name, shape, F32))

        def sem(name):
            return ctx.enter_context(nc.semaphore(name))

        idx = sb("idx", [P, NT], I32)
        pos = sb("pos_or_res", [P, NT, D])
        res = pos
        ident_rev = sb("ident_rev", [P, P + E + D])
        ident, rev = ident_rev[:, 0:P], ident_rev[:, P:P + E]
        halves = ident_rev[:, P + E:P + E + D]
        NF = 16
        by_row = sb("by_row", [NF, P + 3])
        beta_all = sb("beta_all", [NF, 2])
        beta_sel = sb("beta_sel", [NF, 2])
        beta_col = sb("beta_col", [NF, 1])
        row_beta = sb("row_beta", [NF, P])
        row_hi = sb("row_hi", [NF, P])
        row_part = sb("row_part", [NF, P], F32R)
        col_or_hid = sb("col_or_hid", [P, (NB + 4) * CH * P])
        col_in = col_or_hid[0:NF, 0:GW]
        hid = col_or_hid[:, 0:NB * CH * P].rearrange("p (b s) -> p b s", b=NB)
        res_t = col_or_hid[:, NB * CH * P:(NB + 2) * CH * P].rearrange("p (g s) -> p g s", g=2)
        col_or_prt = sb("col_or_prt", [P, 8 * 512], F32R)
        col_part = col_or_prt[0:NF, 0:GW]
        prt = col_or_prt[:, :].rearrange("p (r b s) -> p r b s", r=2, b=4)
        prt_hi, prt_lo = prt[:, 0, :, :], prt[:, 1, :, :]
        bias = sb("bias", [P, GW])
        h0 = sb("h0", [P, NT, D])
        stats1 = sb("stats1", [P, NT, 6])
        mv1 = sb("mv1", [P, NT, 2])
        std1 = sb("std1", [P, NT])
        warm = sb("warm", [P, 1])
        var1 = sb("var1", [P, NT])
        near1 = sb("near1", [P, NT])
        nr = sb("nr", [P, 2, CH])
        rs_last = sb("rs_last", [P, 5, 2])
        rstd1 = sb("rstd1", [P, NT])
        shift1 = sb("shift1", [P, NT])
        xn1 = sb("xn1", [P, NT, D])
        x_or_hid = sb("x_or_hid", [P, 2 * S], F32R)
        xn1_split = x_or_hid[:, 0:S].rearrange("p (t d) -> p t d", t=NT)
        xt = x_or_hid[:, S:2 * S]
        hid_part = x_or_hid[:, :].rearrange("p (b r s) -> p b r s", b=NB, r=2)
        w_nat = sb("w_nat", [D, 3, 2 * D])
        w_t = sb("w_t", [P, WC])
        w_hi = sb("w_hi", [P, WC], F32R)
        w_lo = sb("w_lo", [P, WC], F32R)
        b_nat = sb("b_nat", [2 + NB, P])
        b_col = sb("b_col", [P, 2 + NB])
        bv_all = sb("bv_all", [P, D])
        q_split = sb("q_split", [P, S], F32R)
        k_hi = sb("k_hi", [P, S], F32R)
        k_lo = sb("k_lo", [P, S], F32R)
        v = sb("v", [P, NT, D])
        v_split = sb("v_split", [P, NT, 2 * D], F32R)
        sc = sb("sc", [P, 2, S])
        pmax = sb("pmax", [P, NT, 4])
        pmax2 = sb("pmax2", [P, 2])
        nmax = sb("nmax", [P, NT])
        pr = sb("pr", [P, 4, S])
        psumh = sb("psumh", [P, NT, 2])
        den = sb("den", [P, NT])
        rden = sb("rden", [P, NT])
        ot = sb("ot", [P, 2 * P])
        h1 = sb("h1", [P, NT, D])
        stats2 = sb("stats2", [P, NT, 6])
        mv2 = sb("mv2", [P, NT, 2])
        rs2 = sb("rs2", [P, 5, 2])
        rstd2 = sb("rstd2", [P, NT])
        shift2 = sb("shift2", [P, 2])
        xn2 = sb("xn2", [P, CH, D])
        xn2_split = sb("xn2_split", [P, CH, 2 * D], F32R)
        x2t = sb("x2t", [P, 2, CH * P], F32R)
        rw_nat = sb("rw_nat", [E, 2 * D])
        rb_all = sb("rb_all", [P, E])
        logit = sb("logit", [P, CH, E])
        lmax = sb("lmax", [P, CH])
        tie = sb("tie", [P, CH, E])
        tmax = sb("tmax", [P, CH])
        chosen = sb("chosen", [P, CH, E])
        chosen_t = sb("chosen_t", [E, 2, CH * P], F32R)
        mask_f = sb("mask_f", [E, E * H])
        mask = sb("mask", [E, E * H], F32R)
        w1_nat = sb("w1_nat", [P, E, H])
        w1_hi = sb("w1_hi", [P, E * H], F32R)
        w1_lo = sb("w1_lo", [P, E * H], F32R)
        w2_s = sb("w2_s", [P, NB, D])
        w2_split = sb("w2_split", [P, NB, 2 * D], F32R)
        b2_s = sb("b2_s", [E, D])
        b2_split = sb("b2_split", [E, 2 * D], F32R)

        ps_s = ps("ps_s", [P, NB_S, 512])
        ps_t = ps("ps_t", [P, NB_T, 512])
        ps_o = ps("ps_o", [P, 512])
        ps_f = ps("ps_f", [P, NB_F, 512])

        idx_in, pos_in, const_in = sem("idx_in"), sem("pos_in"), sem("const_in")
        biasf_in, wqkv_in, wexp_in = sem("biasf_in"), sem("wqkv_in"), sem("wexp_in")
        tok_in = [sem(f"tok_in{c}") for c in range(NC)]
        out_sent = sem("out_sent")
        row_ready, biasmm, bias_act, bias_dve = sem("row_ready"), sem("biasmm"), sem("bias_act"), sem("bias_dve")
        wt_turned, wt_ready = sem("wt_turned"), sem("wt_ready")
        col_ready, v_copied, wt_step = sem("col_ready"), sem("v_copied"), sem("wt_step")
        stat_step, rs_step = sem("stat_step"), sem("rs_step")
        var1_ready, std1_ready, rstd1_ready = sem("var1_ready"), sem("std1_ready"), sem("rstd1_ready")
        xn1_hi_ready, xn1_ready, xt_turned, xt_ready = (
            sem("xn1_hi_ready"), sem("xn1_ready"), sem("xt_turned"), sem("xt_ready"))
        q_mm, k_mm, v_mm = sem("q_mm"), sem("k_mm"), sem("v_mm")
        q_hi_done, k_hi_done, q_ready, k_ready, v_ready = (
            sem("q_hi_done"), sem("k_hi_done"), sem("q_ready"), sem("k_ready"), sem("v_ready"))
        expw_ready = sem("expw_ready")
        s_mm = sem("s_mm")
        s_read = sem("s_read")
        pmax2_done, nmax_ready = sem("pmax2_done"), sem("nmax_ready")
        exp_done = sem("exp_done")
        p_turned = sem("p_turned")
        p_hi = sem("p_hi")
        p_lo = sem("p_lo")
        pv_mm = sem("pv_mm")
        ot_ready = sem("ot_ready")
        ot_turned = sem("ot_turned")
        den_done, rden_done, stats2_done = sem("den_done"), sem("rden_done"), sem("stats2_done")
        h1_done = sem("h1_done")
        rstd2_ready, xn2_hi_ready = sem("rstd2_ready"), sem("xn2_hi_ready")
        mv2_ready, xs_ready = sem("mv2_ready"), sem("xs_ready")
        x2_turned, x2t_ready = sem("x2_turned"), sem("x2t_ready")
        logit_mm, chosen_ready, chosen_turned = sem("logit_mm"), sem("chosen_ready"), sem("chosen_turned")
        chosen_t_ready = sem("chosen_t_ready")
        hid_mm, hid_ready, hid_lo_ready = sem("hid_mm"), sem("hid_ready"), sem("hid_lo_ready")
        out_mm, res_t_ready, out_turned, res_done = sem("out_mm"), sem("res_t_ready"), sem("out_turned"), sem("res_done")
        logit_read, choose_step = sem("logit_read"), sem("choose_step")
        dve_step, pool_step, act_step = sem("dve_step"), sem("pool_step"), sem("act_step")

        block = ctx.enter_context(nc.Block())

        BW = [min(512, GW - 512 * j) for j in range(-(-GW // 512))]
        half = S // 2

        s_free, t_free = 4 * NT - LAG + 2, 4 * NT + 3
        stage_bank, turn = {}, 0
        for k in slots:
            m, at = (k - OUT_LAG) // 8, (k - OUT_LAG) % 8
            for use in ([("out", m)] if at == 0 and 0 <= m < NPAIR else []) + stages.get(k, []):
                banks = ["f0", "f1"] + ["s0", "s1"] * (k >= s_free) + ["t0", "t1", "t2"] * (k >= t_free)
                stage_bank[use] = banks[turn % len(banks)]
                turn += 1
        bank_of = {}
        for name, bank, n in (("f", ps_f, NB_F), ("s", ps_s, NB_S), ("t", ps_t, NB_T)):
            for b in range(n):
                bank_of[f"{name}{b}"] = bank[:, b, :]
        bias_bank = [ps_s[:, 0, :], ps_s[:, 1, :], ps_f[:, 1, :]]

        def q_bank(c):
            return ps_t[:, 2, :] if c % 2 else ps_o[:, :]

        def hid_cols(g):
            w = GROUPS[g][1] * P
            return slice(w, 2 * w) if g == TAIL else slice(0, w)

        def f_bank(g, j):
            return bank_of[stage_bank[g, j]]

        @block.sync
        def _(sp):
            sp.dma_start(idx[:, :], x.rearrange("a (p i) -> (a p) i", p=P)).then_inc(idx_in, 16)
            sp.dma_start(ident_rev[:, :], c_ident).then_inc(const_in, 16)
            sp.dma_start(by_row[:, :], c_row).then_inc(biasf_in, 16)
            sp.dma_start(beta_all[:, :], beta.partition_broadcast(NF)).then_inc(biasf_in, 16)
            sp.dma_start(b_nat[0:1, :].rearrange("p (r d) -> p r d", r=2),
                         bq.rearrange("(a r d) -> a r d", a=1, r=1).to_broadcast([1, 2, D])).then_inc(wqkv_in, 16)
            sp.dma_start(b_nat[1:2, :].rearrange("p (r d) -> p r d", r=2),
                         bk.rearrange("(a r d) -> a r d", a=1, r=1).to_broadcast([1, 2, D])).then_inc(wqkv_in, 16)
            sp.dma_start(b_nat[2:2 + NB, :], b1.rearrange("(b e) h -> b (e h)", b=NB)).then_inc(wqkv_in, 16)
            sp.dma_start(pos[:, :, :], c_pos.rearrange("p (i d) -> p i d", d=D)).then_inc(pos_in, 16)
            sp.dma_start(bv_all[:, :], bv.partition_broadcast(P)).then_inc(wexp_in, 16)
            w1_v = w1.rearrange("e d h -> d e h")
            sp.dma_start(w1_nat[0:D, :, :], w1_v).then_inc(wexp_in, 16)
            sp.dma_start(w1_nat[D:2 * D, :, :], w1_v).then_inc(wexp_in, 16)
            sp.dma_start(mask_f[:, :], c_mask).then_inc(wexp_in, 16)
            sp.dma_start(w2_s[:, :, :], w2.rearrange("(b e) h d -> (e h) b d", b=NB)).then_inc(wexp_in, 16)
            sp.dma_start(b2_s[:, :], b2).then_inc(wexp_in, 16)
            sp.dma_start(rb_all[:, :], rb.partition_broadcast(P)).then_inc(wexp_in, 16)
            out_v = out.rearrange("a (p i) d -> (a p) i d", p=P)
            for g, (t0, n) in enumerate(GROUPS):
                sp.wait_ge(res_done, g + 1)
                sp.dma_start(out_v[:, t0:t0 + n, :], res[:, t0:t0 + n, :]).then_inc(out_sent, 16)
            sp.wait_ge(out_sent, 16 * len(GROUPS))

        @block.gpsimd
        def _(pool):
            pool.wait_ge(idx_in, 16)
            for i in range(NT):
                nc.gpsimd.indirect_dma_start(
                    out=h0[:, i, :], out_offset=None, in_=tok_w,
                    in_offset=bass.IndirectOffsetOnAxis(ap=idx[:, i:i + 1], axis=0),
                ).then_inc(tok_in[i // CH], 16)
            own = [0]

            def then_own(ins):
                ins.then_inc(pool_step, 1)
                own[0] += 1
                pool.wait_ge(pool_step, own[0])

            pool.wait_ge(wexp_in, 7 * 16)
            for c in range(NC):
                tiles = slice(CH * c, CH * (c + 1))
                pool.wait_ge(v_copied, c + 1)
                then_own(nc.gpsimd.tensor_tensor(v[:, tiles, :], v[:, tiles, :],
                                                 bv_all[:, :].unsqueeze(1).to_broadcast([P, CH, D]), ALU.add))
                then_own(nc.gpsimd.tensor_copy(v_split[:, tiles, 0:D], v[:, tiles, :]))
                nc.gpsimd.tensor_tensor(v_split[:, tiles, D:2 * D], v[:, tiles, :],
                                        v_split[:, tiles, 0:D].bitcast(F32), ALU.subtract).then_inc(v_ready, 1)
            w1_f = w1_nat[:, :, :].rearrange("p e h -> p (e h)")
            nc.gpsimd.tensor_copy(w1_hi[:, :], w1_f)
            nc.gpsimd.tensor_copy(mask[:, :], mask_f[:, :])
            nc.gpsimd.tensor_copy(w2_split[:, :, 0:D], w2_s[:, :, :])
            then_own(nc.gpsimd.tensor_copy(b2_split[:, 0:D], b2_s[:, :]))
            nc.gpsimd.tensor_tensor(w1_lo[:, :], w1_f, w1_hi[:, :].bitcast(F32), ALU.subtract)
            nc.gpsimd.tensor_tensor(w2_split[:, :, D:2 * D], w2_s[:, :, :], w2_split[:, :, 0:D].bitcast(F32), ALU.subtract)
            nc.gpsimd.tensor_tensor(b2_split[:, D:2 * D], b2_s[:, :], b2_split[:, 0:D].bitcast(F32), ALU.subtract
                                    ).then_inc(expw_ready, 1)

            def hidden_lo(g):
                for b in range(NB):
                    pool.wait_ge(hid_ready, NB * g + b + 1)
                    w = GROUPS[g][1] * P
                    nc.gpsimd.tensor_tensor(hid_part[:, b, 1, 0:w], hid[:, b, 0:w], hid_part[:, b, 0, 0:w].bitcast(F32),
                                            ALU.subtract).then_inc(hid_lo_ready, 1)

            for m in range(NPAIR):
                if m == POOL_HIDDEN[0]:
                    hidden_lo(0)
                if m == POOL_HIDDEN[1]:
                    hidden_lo(1)
                if group_of[m] == TAIL:
                    break
                g = group_of[m]
                tiles = slice(2 * m, 2 * m + 2)
                here = slice(2 * m % CH, 2 * m % CH + 2)
                pool.wait_ge(mv2_ready, m + 1)
                if m >= 2:
                    pool.wait_ge(x2_turned, group_of[m - 2] + 1)
                v2, h2, y, t, u = (rs2[:, r, :] for r in range(5))
                then_own(nc.gpsimd.tensor_scalar(v2, mv2[:, tiles, 1], EPS, None, ALU.add))
                nc.gpsimd.tensor_scalar(h2, v2, -0.5, None, ALU.mult)
                then_own(nc.gpsimd.tensor_scalar(y.bitcast(I32), v2.bitcast(I32), -0.5, RSQRT_MAGIC, ALU.mult, ALU.add))
                for step in range(3):
                    then_own(nc.gpsimd.tensor_tensor(t, y, y, ALU.mult))
                    then_own(nc.gpsimd.tensor_tensor(u, t, h2, ALU.mult))
                    then_own(nc.gpsimd.tensor_scalar(t, u, 1.5, None, ALU.add))
                    then_own(nc.gpsimd.tensor_tensor(rstd2[:, tiles] if step == 2 else y, t, y, ALU.mult))
                for t in range(2):
                    ins = nc.gpsimd.tensor_scalar(xn2[:, here, :][:, t, :], h1[:, 2 * m + t, :], mv2[:, 2 * m + t, 0:1],
                                                  rstd2[:, 2 * m + t:2 * m + t + 1], ALU.subtract, ALU.mult)
                then_own(ins)
                then_own(nc.gpsimd.tensor_copy(xn2_split[:, here, 0:D], xn2[:, here, :]))
                nc.gpsimd.tensor_tensor(xn2_split[:, here, D:2 * D], xn2[:, here, :],
                                        xn2_split[:, here, 0:D].bitcast(F32), ALU.subtract).then_inc(xs_ready, 1)

        @block.scalar
        def _(act):
            act.dma_start(col_in[:, :], c_col).then_inc(biasf_in, 16)
            for r, w in enumerate((wq, wk, wv)):
                act.dma_start(w_nat[:, r, :].rearrange("p (r d) -> p r d", r=2),
                              w.unsqueeze(1).to_broadcast([D, 2, D])).then_inc(wqkv_in, 16)
            act.dma_start(rw_nat[:, :].rearrange("p (r d) -> p r d", r=2),
                          rw.unsqueeze(1).to_broadcast([E, 2, D])).then_inc(wqkv_in, 16)
            act.wait_ge(const_in, 16)
            nc.scalar.activation(warm[:, :], rev[:, 0:1], ACT.Sqrt)
            act.wait_ge(biasf_in, 3 * 16)
            nc.scalar.activation(col_part[:, :], col_in[:, :], ACT.Copy).then_inc(col_ready, 1)

            def bias_piece(j):
                act.wait_ge(biasmm, j + 1)
                nc.scalar.activation(bias[:, 512 * j:512 * j + BW[j]], bias_bank[j % 3][:, 0:BW[j]], ACT.Copy
                                     ).then_inc(bias_act, 1)

            def std(c):
                tiles = slice(CH * c, CH * (c + 1))
                act.wait_ge(var1_ready, c + 1)
                nc.scalar.activation(std1[:, tiles], var1[:, tiles], ACT.Sqrt).then_inc(std1_ready, 1)

            def normalise(c):
                act.wait_ge(rstd1_ready, c + 1)
                for t in range(CH * c, CH * (c + 1)):
                    ins = nc.scalar.activation(xn1[:, t, :], h0[:, t, :], ACT.Identity, bias=shift1[:, t:t + 1],
                                               scale=rstd1[:, t:t + 1])
                ins.then_inc(act_step, 1)

            def x_hi(c):
                tiles = slice(CH * c, CH * (c + 1))
                act.wait_ge(act_step, c + 1)
                nc.scalar.activation(xn1_split[:, tiles, 0:D], xn1[:, tiles, :], ACT.Copy).then_inc(xn1_hi_ready, 1)

            def copy_xt(c):
                act.wait_ge(xt_turned, c + 1)
                nc.scalar.activation(xt[:, c * 512:(c + 1) * 512], ps_t[:, 0, :], ACT.Copy).then_inc(xt_ready, 1)

            def copy_k(c):
                act.wait_ge(k_mm, c + 1)
                nc.scalar.activation(k_hi[:, c * 512:(c + 1) * 512], ps_f[:, 0, :], ACT.Identity, bias=b_col[:, 1:2]
                                     ).then_inc(k_hi_done, 1)

            def copy_q(c):
                act.wait_ge(q_mm, c + 1)
                nc.scalar.activation(q_split[:, c * 512:(c + 1) * 512], q_bank(c), ACT.Identity, bias=b_col[:, 0:1]
                                     ).then_inc(q_hi_done, 1)

            def copy_v(c):
                act.wait_ge(v_mm, c + 1)
                nc.scalar.activation(v[:, CH * c:CH * (c + 1), :], ps_t[:, 1, 0:CH * D].rearrange("p (t d) -> p t d", d=D),
                                     ACT.Copy).then_inc(v_copied, 1)

            bias_piece(1)
            std(0)
            normalise(0)
            x_hi(0)
            bias_piece(3)
            std(1)
            copy_xt(0)
            normalise(1)
            std(2)
            x_hi(1)
            copy_k(0)
            copy_q(0)
            copy_xt(1)
            normalise(2)
            std(3)
            x_hi(2)
            copy_k(1)
            bias_piece(5)
            bias_piece(7)
            copy_xt(2)
            normalise(3)
            x_hi(3)
            copy_k(2)
            copy_xt(3)
            copy_q(1)
            copy_k(3)
            copy_v(0)
            copy_v(1)

            def exp_half(t, a):
                m = t // 2
                if a == 0:
                    act.wait_ge(nmax_ready, t + 1)
                if m >= 2:
                    act.wait_ge(p_turned, 8 * (m - 2) + 4 * (a + 1))
                cols = slice(a * half, (a + 1) * half)
                nc.scalar.activation(pr[:, t % 4, cols], sc[:, t % 2, cols], ACT.Exp, bias=nmax[:, t:t + 1],
                                     accum_out=psumh[:, t, a:a + 1]).then_inc(exp_done, 1)

            def copy_hi(k):
                act.wait_ge(p_turned, k + 1)
                if k >= 4:
                    act.wait_ge(pv_mm, k - 3)
                nc.scalar.activation(prt_hi[:, k % 4, :], ps_t[:, k % NB_T, :], ACT.Copy).then_inc(p_hi, 1)

            def copy_out(m):
                act.wait_ge(pv_mm, 8 * (m + 1))
                if m >= 1:
                    act.wait_ge(ot_turned, m)
                nc.scalar.activation(ot[:, :], ps_o[:, 0:2 * P], ACT.Copy).then_inc(ot_ready, 1)

            def expert(g, j):
                t0, n = GROUPS[g]
                w = n * P
                cols = hid_cols(g)
                bank = f_bank(g, j)
                if j == 0:
                    act.wait_ge(x2_turned, g + 1)
                    if g >= 2:
                        act.wait_ge(hid_mm, NB * (g - 1))
                    nc.scalar.activation(x2t[:, g % 2, 0:w], bank[:, 0:w], ACT.Copy).then_inc(x2t_ready, 1)
                elif j == 2:
                    act.wait_ge(chosen_turned, g + 1)
                    if g >= 2:
                        act.wait_ge(out_mm, g - 1)
                    nc.scalar.activation(chosen_t[:, g % 2, 0:w], bank[0:E, 0:w], ACT.Copy).then_inc(chosen_t_ready, 1)
                elif 3 <= j <= 6:
                    b = j - 3
                    act.wait_ge(hid_mm, NB * g + b + 1)
                    if g >= 1:
                        act.wait_ge(out_mm, g if g < TAIL else g - 1)
                        act.wait_ge(hid_lo_ready, NB * (g - 1) + b + 1)
                    nc.scalar.activation(hid[:, b, 0:w], bank[:, 0:w], ACT.Relu, bias=b_col[:, 2 + b:3 + b])
                    nc.scalar.activation(hid_part[:, b, 0, cols], bank[:, 0:w], ACT.Relu, bias=b_col[:, 2 + b:3 + b]
                                         ).then_inc(hid_ready, 1)
                elif j == 7:
                    act.wait_ge(out_mm, g + 1)
                    nc.scalar.activation(res_t[:, g % 2, 0:w], bank[:, 0:w], ACT.Copy).then_inc(res_t_ready, 1)

            def normalise_last():
                act.wait_ge(rstd2_ready, 1)
                for t in range(NT - 2, NT):
                    ins = nc.scalar.activation(xn2[:, t % CH, :], h1[:, t, :], ACT.Identity, bias=shift2[:, t % 2:t % 2 + 1],
                                               scale=rstd2[:, t:t + 1])
                ins.then_inc(act_step, 1)
                act.wait_ge(act_step, NC + 1)
                nc.scalar.activation(xn2_split[:, 2:4, 0:D], xn2[:, 2:4, :], ACT.Copy).then_inc(xn2_hi_ready, 1)

            for k in slots:
                if k in late_v:
                    copy_v(late_v[k])
                if k in late_q:
                    copy_q(late_q[k])
                m, at = (k - OUT_LAG + 1) // 8, (k - OUT_LAG + 1) % 8
                if at == 0 and 0 <= m < NPAIR:
                    copy_out(m)
                for g, j in stages.get(k, []):
                    expert(g, j)
                if k == LAST_AT:
                    normalise_last()
                if 0 <= k < 4 * NT:
                    copy_hi(k)
                m, at = (k + LAG - EXP_LAG) // 8, (k + LAG - EXP_LAG) % 8
                if at % 2 == 0 and 0 <= m < NPAIR:
                    exp_half(2 * m + at // 4, at // 2 % 2)

        @block.tensor
        def _(pe):
            pe.wait_ge(const_in, 16)
            pe.wait_ge(wqkv_in, 7 * 16)
            for r in range(3):
                nc.tensor.transpose(ps_t[:, 0, r * D:(r + 1) * D], w_nat[:, r, :], ident[0:D, 0:D])
            nc.tensor.transpose(ps_t[:, 0, 3 * D:3 * D + E], rw_nat[:, :], ident[0:E, 0:E])
            nc.tensor.transpose(ps_t[:, 0, 3 * D + E:3 * D + E + 2 + NB], b_nat[:, :], ident[0:2 + NB, 0:2 + NB]
                                ).then_inc(wt_turned, 1)
            pe.wait_ge(row_ready, 1)
            pe.wait_ge(col_ready, 1)

            def bias_piece(j):
                if j >= 3:
                    i = j - 3
                    pe.wait_ge(bias_act if i % 2 else bias_dve, i // 2 + 1)
                nc.tensor.matmul(bias_bank[j % 3][:, 0:BW[j]], row_part[:, :],
                                 col_part[:, 512 * j:512 * j + BW[j]], start=True, stop=True).then_inc(biasmm, 1)

            def turn_x(c):
                pe.wait_ge(xn1_ready, c + 1)
                if c == 0:
                    pe.wait_ge(wt_ready, 1)
                for t in range(CH):
                    mm = nc.tensor.transpose(ps_t[:, 0, t * P:(t + 1) * P],
                                             xn1_split[:, CH * c + t, :].bitcast(F32), ident)
                mm.then_inc(xt_turned, 1)

            def make_k(c):
                cols = slice(c * 512, (c + 1) * 512)
                pe.wait_ge(xt_ready, c + 1)
                if c >= 1:
                    pe.wait_ge(k_ready, c)
                nc.tensor.matmul(ps_f[:, 0, :], w_hi[:, WK], xt[:, cols], start=True, stop=False)
                nc.tensor.matmul(ps_f[:, 0, :], w_lo[:, WK], xt[:, cols], start=False, stop=True).then_inc(k_mm, 1)

            def make_q(c):
                cols = slice(c * 512, (c + 1) * 512)
                if c >= 2:
                    pe.wait_ge(q_ready, c - 1)
                nc.tensor.matmul(q_bank(c), w_hi[:, WQ], xt[:, cols], start=True, stop=False)
                nc.tensor.matmul(q_bank(c), w_lo[:, WQ], xt[:, cols], start=False, stop=True).then_inc(q_mm, 1)

            def make_v(c):
                if c >= 1:
                    pe.wait_ge(v_copied, c)
                for t in range(CH):
                    x_t = xt[:, (CH * c + t) * P:(CH * c + t + 1) * P]
                    o = ps_t[:, 1, t * D:(t + 1) * D]
                    nc.tensor.matmul(o, x_t, w_hi[:, WV], start=True, stop=False)
                    mm = nc.tensor.matmul(o, x_t, w_lo[:, WV], start=False, stop=True)
                mm.then_inc(v_mm, 1)

            def scores(u):
                t, b = u // 4, u % 4
                if u == 0:
                    pe.wait_ge(q_ready, 1)
                    pe.wait_ge(bias_act, len(BW) // 2)
                    pe.wait_ge(bias_dve, (len(BW) + 1) // 2)
                if t == 0:
                    pe.wait_ge(k_ready, b + 1)
                if t > 0 and t % CH == 0 and b == 0:
                    pe.wait_ge(q_ready, t // CH + 1)
                if u >= NB_S:
                    pe.wait_ge(s_read, u - NB_S + 1)
                queries = q_split[:, t * P:(t + 1) * P]
                keys = slice(b * 512, (b + 1) * 512)
                nc.tensor.matmul(ps_s[:, u % NB_S, :], queries, k_hi[:, keys], start=True, stop=False)
                nc.tensor.matmul(ps_s[:, u % NB_S, :], queries, k_lo[:, keys], start=False, stop=True).then_inc(s_mm, 1)

            def turn(k):
                m, q = k // 8, k % 8
                if q % 4 == 0:
                    pe.wait_ge(exp_done, 4 * m + 3 + q // 4)
                if k >= NB_T:
                    pe.wait_ge(p_lo, k - NB_T + 1)
                if k == 0:
                    pe.wait_ge(v_copied, NC)
                    pe.wait_ge(q_ready, NC)
                for b in range(2):
                    for t in range(2):
                        mm = nc.tensor.transpose(ps_t[:, k % NB_T, (2 * b + t) * P:(2 * b + t + 1) * P],
                                                 pr[:, (2 * m + t) % 4, (2 * q + b) * P:(2 * q + b + 1) * P], ident)
                mm.then_inc(p_turned, 1)

            def times_v(k):
                m, q = k // 8, k % 8
                pe.wait_ge(p_lo, k + 1)
                if k == 0:
                    pe.wait_ge(v_ready, NC)
                if q == 0 and m >= 1:
                    pe.wait_ge(ot_ready, m)
                for b in range(2):
                    cols, values = slice(2 * b * P, 2 * (b + 1) * P), v_split[:, 2 * q + b, :]
                    nc.tensor.matmul(ps_o[:, 0:2 * P], values, prt_hi[:, k % 4, cols],
                                     start=(q == 0 and b == 0), stop=False)
                    mm = nc.tensor.matmul(ps_o[:, 0:2 * P], values, prt_lo[:, k % 4, cols],
                                          start=False, stop=(q == 7 and b == 1))
                mm.then_inc(pv_mm, 1)

            last_read = {"f0": (k_ready, NC), "f1": (bias_dve, (len(BW) + 1) // 2)}
            last_read.update({f"s{b}": (s_read, 4 * NT) for b in range(NB_S)})
            last_read.update({f"t{b}": (p_lo, 4 * NT) for b in range(NB_T)})

            def turn_out(m):
                pe.wait_ge(ot_ready, m + 1)
                bank = stage_bank["out", m]
                pe.wait_ge(*last_read[bank])
                for t in range(2):
                    mm = nc.tensor.matmul(bank_of[bank][:, t * D:(t + 1) * D], ot[:, t * P:(t + 1) * P], halves,
                                          start=True, stop=True)
                mm.then_inc(ot_turned, 1)
                last_read[bank] = (h1_done, m + 1)

            def expert(g, j):
                t0, n = GROUPS[g]
                w = n * P
                cols = hid_cols(g)
                bank = f_bank(g, j)
                x_all = x2t[:, g % 2, :]
                pe.wait_ge(*last_read[stage_bank[g, j]])
                if j == 0:
                    pe.wait_ge(xs_ready, (t0 + n) // 2)
                    for t in range(n):
                        mm = nc.tensor.transpose(bank[:, t * P:(t + 1) * P], xn2_split[:, (t0 + t) % CH, :].bitcast(F32), ident)
                    mm.then_inc(x2_turned, 1)
                    last_read[stage_bank[g, j]] = (x2t_ready, g + 1)
                elif j == 1:
                    pe.wait_ge(x2t_ready, g + 1)
                    if g == 0:
                        pe.wait_ge(expw_ready, 1)
                    for t in range(n):
                        x_t = x_all[:, t * P:(t + 1) * P]
                        nc.tensor.matmul(bank[:, t * E:(t + 1) * E], x_t, w_hi[:, WR], start=True, stop=False)
                        mm = nc.tensor.matmul(bank[:, t * E:(t + 1) * E], x_t, w_lo[:, WR], start=False, stop=True)
                    mm.then_inc(logit_mm, 1)
                    last_read[stage_bank[g, j]] = (logit_read, g + 1)
                elif j == 2:
                    pe.wait_ge(chosen_ready, g + 1)
                    for t in range(n):
                        mm = nc.tensor.transpose(bank[0:E, t * P:(t + 1) * P], chosen[:, t, :], ident)
                    mm.then_inc(chosen_turned, 1)
                    last_read[stage_bank[g, j]] = (chosen_t_ready, g + 1)
                elif j <= 6:
                    b = j - 3
                    if b == 0:
                        pe.wait_ge(chosen_t_ready, g + 1)
                    rows = slice(b * P, (b + 1) * P)
                    nc.tensor.matmul(bank[:, 0:w], w1_hi[:, rows], x_all[:, 0:w], start=True, stop=False)
                    nc.tensor.matmul(bank[:, 0:w], w1_lo[:, rows], x_all[:, 0:w], start=False, stop=False)
                    nc.tensor.matmul(bank[:, 0:w], mask[:, rows], chosen_t[:, g % 2, 0:w],
                                     start=False, stop=True).then_inc(hid_mm, 1)
                    last_read[stage_bank[g, j]] = (hid_ready, NB * g + b + 1)
                elif j == 7:
                    nc.tensor.matmul(bank[:, 0:w], b2_split[:, :], chosen_t[:, g % 2, 0:w], start=True, stop=False)
                    for b in range(NB):
                        pe.wait_ge(hid_lo_ready, NB * g + b + 1)
                        nc.tensor.matmul(bank[:, 0:w], w2_split[:, b, :], hid_part[:, b, 0, cols], start=False, stop=False)
                        mm = nc.tensor.matmul(bank[:, 0:w], w2_split[:, b, :], hid_part[:, b, 1, cols],
                                              start=False, stop=(b == NB - 1))
                    mm.then_inc(out_mm, 1)
                    last_read[stage_bank[g, j]] = (res_t_ready, g + 1)
                else:
                    pe.wait_ge(res_t_ready, g + 1)
                    for t in range(n):
                        mm = nc.tensor.matmul(bank[:, t * D:(t + 1) * D], res_t[:, g % 2, t * P:(t + 1) * P], halves,
                                              start=True, stop=True)
                    mm.then_inc(out_turned, 1)
                    last_read[stage_bank[g, j]] = (res_done, g + 1)

            for j in range(5):
                bias_piece(j)
            turn_x(0)
            bias_piece(5)
            make_k(0)
            make_q(0)
            bias_piece(6)
            turn_x(1)
            make_k(1)
            bias_piece(7)
            turn_x(2)
            scores(0)
            make_k(2)
            scores(1)
            turn_x(3)
            make_q(1)
            make_k(3)
            scores(2)
            make_v(0)
            make_v(1)

            for k in slots:
                if k in late_v:
                    make_v(late_v[k])
                if k in late_q:
                    make_q(late_q[k])
                m, at = (k - OUT_LAG) // 8, (k - OUT_LAG) % 8
                if at == 0 and 0 <= m < NPAIR:
                    turn_out(m)
                for g, j in stages.get(k, []):
                    expert(g, j)
                if 0 <= k < 4 * NT:
                    turn(k)
                if EARLY <= k + LAG < 4 * NT:
                    scores(k + LAG)
                if 3 <= k < 4 * NT + 3:
                    times_v(k - 3)

        @block.vector
        def _(dve):
            steps = [0]

            def then_own(ins):
                ins.then_inc(dve_step, 1)
                steps[0] += 1
                dve.wait_ge(dve_step, steps[0])

            def newton_1(t, near, var):
                return nc.vector.tensor_tensor(t, near, var, ALU.mult)

            def newton_2(u, t, near):
                return nc.vector.scalar_tensor_tensor(u, t, -0.5, near, ALU.mult, ALU.mult)

            def newton_3(dst, u, near):
                return nc.vector.scalar_tensor_tensor(dst, u, 1.5, near, ALU.add, ALU.mult)

            dve.wait_ge(biasf_in, 3 * 16)
            then_own(nc.vector.tensor_tensor(beta_sel[:, :], beta_all[:, :], by_row[:, P + 1:P + 3], ALU.mult))
            then_own(nc.vector.tensor_reduce(beta_col[:, :], beta_sel[:, :], AX.X, ALU.add))
            then_own(nc.vector.tensor_scalar(row_beta[:, :], by_row[:, 0:P], beta_col[:, 0:1], None, ALU.mult))
            then_own(nc.vector.tensor_copy(row_part[:, :], row_beta[:, :]))
            then_own(nc.vector.tensor_scalar(row_hi[:, :], row_part[:, :].bitcast(F32), by_row[:, P:P + 1], None, ALU.mult))
            nc.vector.tensor_tensor(row_part[:, :], row_beta[:, :], row_hi[:, :], ALU.subtract).then_inc(row_ready, 1)

            def add_position(c):
                tiles = slice(CH * c, CH * (c + 1))
                if c == 0:
                    dve.wait_ge(pos_in, 16)
                dve.wait_ge(tok_in[c], CH * 16)
                nc.vector.tensor_tensor(h0[:, tiles, :], h0[:, tiles, :], pos[:, tiles, :], ALU.add
                                        ).then_inc(stat_step, 1)

            def chunk_stats(c):
                dve.wait_ge(stat_step, 3 * c + 1)
                for t in range(CH * c, CH * (c + 1)):
                    st = nc.vector.bn_stats(stats1[:, t, :], h0[:, t, :])
                st.then_inc(stat_step, 1)

            def chunk_moments(c):
                dve.wait_ge(stat_step, 3 * c + 2)
                for t in range(CH * c, CH * (c + 1)):
                    st = nc.vector.bn_aggr(mv1[:, t, :], stats1[:, t, :])
                st.then_inc(stat_step, 1)

            def chunk_var(c):
                tiles = slice(CH * c, CH * (c + 1))
                dve.wait_ge(stat_step, 3 * c + 3)
                nc.vector.tensor_scalar(var1[:, tiles], mv1[:, tiles, 1], EPS, None, ALU.add).then_inc(var1_ready, 1)

            def chunk_reciprocal(c):
                tiles = slice(CH * c, CH * (c + 1))
                dve.wait_ge(std1_ready, c + 1)
                nc.vector.reciprocal(near1[:, tiles], std1[:, tiles]).then_inc(rs_step, 1)

            def chunk_newton(c):
                tiles = slice(CH * c, CH * (c + 1))
                dve.wait_ge(rs_step, c + 1)
                then_own(newton_1(nr[:, 0, 0:CH], near1[:, tiles], var1[:, tiles]))
                then_own(newton_2(nr[:, 1, 0:CH], nr[:, 0, 0:CH], near1[:, tiles]))
                then_own(newton_3(rstd1[:, tiles], nr[:, 1, 0:CH], near1[:, tiles]))
                nc.vector.scalar_tensor_tensor(shift1[:, tiles], mv1[:, tiles, 0], -1.0, rstd1[:, tiles],
                                               ALU.mult, ALU.mult).then_inc(rstd1_ready, 1)

            def x_lo(c):
                tiles = slice(CH * c, CH * (c + 1))
                dve.wait_ge(xn1_hi_ready, c + 1)
                nc.vector.tensor_tensor(xn1_split[:, tiles, D:2 * D], xn1[:, tiles, :],
                                        xn1_split[:, tiles, 0:D].bitcast(F32), ALU.subtract).then_inc(xn1_ready, 1)

            def split_k(c):
                cols = slice(c * 512, (c + 1) * 512)
                dve.wait_ge(k_hi_done, c + 1)
                nc.vector.scalar_tensor_tensor(k_lo[:, cols], ps_f[:, 0, :], b_col[:, 1:2], k_hi[:, cols].bitcast(F32),
                                               ALU.add, ALU.subtract).then_inc(k_ready, 1)

            def split_q(c):
                cols = slice(c * 512, (c + 1) * 512)
                dve.wait_ge(q_hi_done, c + 1)
                nc.vector.scalar_tensor_tensor(q_split[D:2 * D, cols], q_bank(c)[D:2 * D, :], b_col[D:2 * D, 0:1],
                                               q_split[D:2 * D, cols].bitcast(F32), ALU.add, ALU.subtract
                                               ).then_inc(q_ready, 1)

            def bias_piece(j):
                dve.wait_ge(biasmm, j + 1)
                nc.vector.tensor_copy(bias[:, 512 * j:512 * j + BW[j]], bias_bank[j % 3][:, 0:BW[j]]).then_inc(bias_dve, 1)

            add_position(0)
            dve.wait_ge(wt_turned, 1)
            chunk_stats(0)
            for r in range(2):
                nc.vector.tensor_scalar(w_t[:, 2 * D * r:2 * D * (r + 1)].rearrange("p (s e) -> p s e", s=2),
                                        ps_t[:, 0, r * D:(r + 1) * D].unsqueeze(1).to_broadcast([P, 2, D]),
                                        1.0 if r else D ** -0.5, None, ALU.mult)
            nc.vector.tensor_copy(w_t[:, 4 * D:WC], ps_t[:, 0, 2 * D:3 * D + E])
            nc.vector.tensor_scalar(b_col[:, 0:1], ps_t[:, 0, 3 * D + E:3 * D + E + 1], D ** -0.5, None, ALU.mult)
            nc.vector.tensor_copy(b_col[:, 1:2 + NB], ps_t[:, 0, 3 * D + E + 1:3 * D + E + 2 + NB]).then_inc(wt_step, 1)
            chunk_moments(0)
            dve.wait_ge(wt_step, 1)
            nc.vector.tensor_copy(w_hi[:, :], w_t[:, :]).then_inc(wt_step, 1)
            chunk_var(0)
            dve.wait_ge(wt_step, 2)
            nc.vector.tensor_tensor(w_lo[:, :], w_t[:, :], w_hi[:, :].bitcast(F32), ALU.subtract).then_inc(wt_ready, 1)
            chunk_reciprocal(0)
            bias_piece(0)
            chunk_newton(0)
            add_position(1)
            bias_piece(2)
            chunk_stats(1)
            chunk_moments(1)
            chunk_var(1)
            x_lo(0)
            chunk_reciprocal(1)
            chunk_newton(1)
            add_position(2)
            bias_piece(4)
            chunk_stats(2)
            chunk_moments(2)
            chunk_var(2)
            x_lo(1)
            chunk_reciprocal(2)
            split_k(0)
            chunk_newton(2)
            add_position(3)
            split_q(0)
            chunk_stats(3)
            bias_piece(6)
            chunk_moments(3)
            chunk_var(3)
            x_lo(2)
            chunk_reciprocal(3)
            split_k(1)
            chunk_newton(3)
            def add_bias(u):
                t, b = u // 4, u % 4
                dve.wait_ge(s_mm, u + 1)
                if t >= 2:
                    dve.wait_ge(exp_done, 2 * (t - 2) + b // 2 + 1)
                b0 = (NT - 1 - t) * P + b * 512
                nc.vector.tensor_tensor_reduce(sc[:, t % 2, b * 512:(b + 1) * 512], ps_s[:, u % NB_S, :],
                                               bias[:, b0:b0 + 512], 1.0, -3.0e38, ALU.add, ALU.max,
                                               pmax[:, t, b:b + 1]).then_inc(s_read, 1)

            add_bias(0)
            x_lo(3)
            split_k(2)
            add_bias(1)
            split_q(1)
            split_k(3)
            add_bias(2)

            def half_max(t):
                dve.wait_ge(s_read, 4 * t + 4)
                nc.vector.tensor_tensor(pmax2[:, :], pmax[:, t, 0:2], pmax[:, t, 2:4], ALU.max).then_inc(pmax2_done, 1)

            def row_max(t):
                dve.wait_ge(pmax2_done, t + 1)
                nc.vector.tensor_scalar(nmax[:, t:t + 1], pmax2[:, 0:1], pmax2[:, 1:2], -1.0,
                                        ALU.max, ALU.mult).then_inc(nmax_ready, 1)

            def copy_lo(k):
                dve.wait_ge(p_hi, k + 1)
                if k >= 4:
                    dve.wait_ge(pv_mm, k - 3)
                nc.vector.tensor_tensor(prt_lo[:, k % 4, :], ps_t[:, k % NB_T, :], prt_hi[:, k % 4, :].bitcast(F32),
                                        ALU.subtract).then_inc(p_lo, 1)

            def pair_sum(m):
                dve.wait_ge(exp_done, 4 * m + 4)
                tiles = slice(2 * m, 2 * m + 2)
                nc.vector.tensor_tensor(den[:, tiles], psumh[:, tiles, 0], psumh[:, tiles, 1], ALU.add).then_inc(den_done, 1)

            def pair_reciprocal(m):
                dve.wait_ge(den_done, m + 1)
                tiles = slice(2 * m, 2 * m + 2)
                nc.vector.reciprocal(rden[:, tiles], den[:, tiles]).then_inc(rden_done, 1)

            def pair_residual(m):
                dve.wait_ge(rden_done, m + 1)
                dve.wait_ge(ot_turned, m + 1)
                bank = bank_of[stage_bank["out", m]]
                for t in range(2):
                    i = 2 * m + t
                    ins = nc.vector.scalar_tensor_tensor(h1[:, i, :], bank[:, t * D:(t + 1) * D], rden[:, i:i + 1],
                                                         h0[:, i, :], ALU.mult, ALU.add)
                ins.then_inc(h1_done, 1)

            def pair_stats(m):
                dve.wait_ge(h1_done, m + 1)
                for t in range(2):
                    ins = nc.vector.bn_stats(stats2[:, 2 * m + t, :], h1[:, 2 * m + t, :])
                ins.then_inc(stats2_done, 1)

            def pair_moments(m):
                dve.wait_ge(stats2_done, m + 1)
                for t in range(2):
                    ins = nc.vector.bn_aggr(mv2[:, 2 * m + t, :], stats2[:, 2 * m + t, :])
                ins.then_inc(mv2_ready, 1)

            def last_rsqrt():
                tiles = slice(NT - 2, NT)
                v2, y, t, u, y2 = (rs_last[:, r, :] for r in range(5))
                dve.wait_ge(mv2_ready, NPAIR)
                then_own(nc.vector.tensor_scalar(v2, mv2[:, tiles, 1], EPS, None, ALU.add))
                then_own(nc.vector.tensor_scalar(y.bitcast(I32), v2.bitcast(I32), -0.5, RSQRT_MAGIC, ALU.mult, ALU.add))
                for near, dst in ((y, y2), (y2, y), (y, rstd2[:, tiles])):
                    then_own(newton_1(t, near, v2))
                    then_own(newton_2(u, t, near))
                    then_own(newton_3(dst, u, near))
                nc.vector.scalar_tensor_tensor(shift2[:, :], mv2[:, tiles, 0], -1.0, rstd2[:, tiles],
                                               ALU.mult, ALU.mult).then_inc(rstd2_ready, 1)
                dve.wait_ge(xn2_hi_ready, 1)
                dve.wait_ge(x2_turned, GROUPS.index((8, 4)) + 1)
                nc.vector.tensor_tensor(xn2_split[:, 2:4, D:2 * D], xn2[:, 2:4, :],
                                        xn2_split[:, 2:4, 0:D].bitcast(F32), ALU.subtract).then_inc(xs_ready, 1)

            def expert(g, j):
                t0, n = GROUPS[g]
                w = n * P
                cols = hid_cols(g)
                if j == 1:
                    dve.wait_ge(logit_mm, g + 1)
                    nc.vector.tensor_tensor(logit[:, 0:n, :],
                                            f_bank(g, j)[:, 0:n * E].rearrange("p (t e) -> p t e", e=E),
                                            rb_all[:, :].unsqueeze(1).to_broadcast([P, n, E]), ALU.add
                                            ).then_inc(logit_read, 1)
                elif 3 <= j <= 6 and g >= 2:
                    b = j - 3
                    dve.wait_ge(hid_ready, NB * g + b + 1)
                    nc.vector.tensor_tensor(hid_part[:, b, 1, cols], hid[:, b, 0:w], hid_part[:, b, 0, cols].bitcast(F32),
                                            ALU.subtract).then_inc(hid_lo_ready, 1)
                elif j == 8:
                    dve.wait_ge(out_turned, g + 1)
                    nc.vector.scalar_tensor_tensor(res[:, t0:t0 + n, :], f_bank(g, j)[:, 0:n * D].rearrange("p (t d) -> p t d", d=D),
                                                   0.0, h1[:, t0:t0 + n, :], ALU.max, ALU.add).then_inc(res_done, 1)

            def choose(g, step):
                t0, n = GROUPS[g]
                lg, ti, ch = logit[:, 0:n, :], tie[:, 0:n, :], chosen[:, 0:n, :]
                if step == 0:
                    dve.wait_ge(logit_read, g + 1)
                    ins = nc.vector.tensor_reduce(lmax[:, 0:n], lg, AX.X, ALU.max)
                else:
                    dve.wait_ge(choose_step, 3 * g + step)
                if step == 1:
                    for t in range(n):
                        ins = nc.vector.scalar_tensor_tensor(tie[:, t, :], logit[:, t, :], lmax[:, t:t + 1], rev,
                                                             ALU.is_equal, ALU.mult)
                elif step == 2:
                    ins = nc.vector.tensor_reduce(tmax[:, 0:n], ti, AX.X, ALU.max)
                if step < 3:
                    ins.then_inc(choose_step, 1)
                else:
                    nc.vector.tensor_tensor(ch, ti, tmax[:, 0:n].unsqueeze(2).to_broadcast([P, n, E]),
                                            ALU.is_equal).then_inc(chosen_ready, 1)

            for k in slots:
                if k in late_q:
                    split_q(late_q[k])
                for g, slots_of in enumerate(STAGE_SLOTS):
                    if 1 <= k - slots_of[1] <= 4:
                        choose(g, k - slots_of[1] - 1)
                u = k + LAG
                if EARLY <= u < 4 * NT:
                    add_bias(u)
                    if u % 4 == 3:
                        half_max(u // 4)
                if 0 <= k < 4 * NT:
                    copy_lo(k)
                if 0 <= u < 4 * NT and u % 4 == 3:
                    row_max(u // 4)
                for at, step in ((OUT_LAG - 2, pair_sum), (OUT_LAG - 1, pair_reciprocal), (OUT_LAG, pair_residual),
                                 (OUT_LAG + 1, pair_stats), (OUT_LAG + 2, pair_moments)):
                    if (k - at) % 8 == 0 and 0 <= (k - at) // 8 < NPAIR:
                        step((k - at) // 8)
                if k == LAST_AT:
                    last_rsqrt()
                for g, j in stages.get(k, []):
                    expert(g, j)


_INS = ["x", "L0_tok_W", "L0_attn_Wq", "L0_attn_bq", "L0_attn_Wk", "L0_attn_bk", "L0_attn_Wv", "L0_attn_bv",
        "L0_attn_beta", "L0_ffn_router_w", "L0_ffn_router_b", "L0_ffn_W1", "L0_ffn_b1", "L0_ffn_W2", "L0_ffn_b2"]


def kernel(**inputs):
    import numpy as _np
    import concourse.bacc as _bacc
    from concourse import mybir as _mybir
    from concourse.bass_utils import run_bass_kernel_spmd as _run

    nc = _bacc.Bacc("TRN2", target_bir_lowering=False, num_devices=1)
    arrays, args = {}, []
    host = {name: _np.ascontiguousarray(inputs[name]) for name in _INS}
    host.update({name: _np.ascontiguousarray(a) for name, a in tables().items()})
    for name, a in host.items():
        arrays[f"in_{name}"] = a
        args.append(nc.dram_tensor(f"in_{name}", a.shape, _mybir.dt.from_np(a.dtype), kind="ExternalInput").ap())
    args.append(nc.dram_tensor("out_0", (1, S, D), _mybir.dt.float32, kind="ExternalOutput").ap())
    build(nc, *args)
    r = _run(nc, [arrays], core_ids=[0])
    return r.results[0]["out_0"]
```

```python
from contextlib import ExitStack

import numpy as np

import concourse.bass as bass
from concourse import mybir

ALU = mybir.AluOpType
ACT = mybir.ActivationFunctionType
F32 = mybir.dt.float32
F32R = mybir.dt.float32r
BF16 = mybir.dt.bfloat16
I32 = mybir.dt.int32
AX = mybir.AxisListType

P = 128
S, D = 2048, 64
NT = S // P
CH = 4
NC = NT // CH
E, H = 32, 16
NB = E * H // P
EPS = 1e-5
SCALES = (24.0, 720.0)
BIG = 2.0 ** 100
RSQRT_MAGIC = 1597463007.0
GROUPS = [(0, 4), (4, 4), (8, 4), (12, 2), (14, 2)]
STAGE_SLOTS = [[29, 31, 38, 41, 43, 44, 48, 51, 56],
               [48, 50, 56, 57, 59, 60, 62, 65, 69],
               [61, 65, 69, 72, 73, 74, 75, 77, 84],
               [68, 69, 75, 80, 81, 82, 83, 88, 91],
               [74, 75, 81, 83, 85, 88, 89, 90, 100]]
ACT_STAGES, DVE_STAGES = (0, 2, 3, 4, 5, 6, 7), (1, 3, 4, 5, 6, 8)
ACT_SLOTS = [[29, 38, 41, 43, 44, 48, 51],
               [48, 56, 57, 59, 60, 62, 65],
               [61, 69, 72, 73, 74, 75, 77],
               [68, 75, 80, 81, 82, 83, 88],
               [74, 81, 83, 85, 88, 89, 90]]
DVE_SLOTS = [[31, 41, 43, 44, 48, 56],
               [50, 57, 59, 60, 62, 69],
               [65, 72, 73, 74, 75, 86],
               [69, 80, 81, 82, 83, 91],
               [75, 83, 85, 88, 89, 100]]
CHOOSE_SLOTS = [[32, 33, 34, 35], [51, 52, 53, 54], [66, 67, 68, 69], [70, 71, 72, 73], [76, 77, 78, 79]]
EARLY = 3
LATE_QV = [4, 6, 5, 7]
LAG = 13
NB_S, NB_T, NB_F = 2, 3, 2
LATE_HID = 2
POOL_HIDDEN = [4, 6]
EXP_AT = [6, 8, 10, 13]
COPY_OUT_AT = 10
PAIR_AT = [10, 11, 12, 13, 14]
OUT_LAG = 13
LATE = 6
LATE_SLOTS = [[64, 65, 66], [71, 72, 73]]


def tables():
    d = np.arange(D)
    inv = np.power(10000.0, -((d - d % 2) / D)).astype(np.float32)
    angle = (np.arange(S, dtype=np.float32)[:, None] * inv).astype(np.float64)
    pos = np.where(d % 2 == 0, np.sin(angle), np.cos(angle)).astype(np.float32)
    w = 2.0 * np.pi / np.array(SCALES)[:, None]
    row = w * (NT * np.arange(P))[None, :]
    col = w * (NT * np.arange(P)[None, :] + np.arange(1 - NT, NT)[:, None]).reshape(1, -1)
    by_row = np.concatenate([np.cos(row), np.sin(row)]).astype(np.float32)
    by_col = np.concatenate([np.cos(col), np.sin(col)]).astype(np.float32)
    ident = np.eye(P, dtype=np.float32)
    rev = np.broadcast_to((E - np.arange(E)).astype(np.float32), (P, E))
    mask = np.where(np.arange(E)[:, None] == np.arange(E * H)[None, :] // H, 0.0, -BIG).astype(np.float32)
    col_hi = ((by_col.view(np.uint32) + np.uint32(0x800)) & np.uint32(0xFFFFF000)).view(np.float32)
    is_lo = np.repeat([0.0, 1.0], 8)[:, None]
    is_scale = np.tile(np.eye(2), (8, 1))
    return {
        "c_pos": pos.reshape(P, NT * D),
        "c_row": np.concatenate([np.tile(by_row, (4, 1)), is_lo, is_scale], axis=1).astype(np.float32),
        "c_col": np.tile(np.concatenate([col_hi, by_col - col_hi]), (2, 1)).astype(np.float32),
        "c_ident": np.concatenate([ident, rev, ident[:, 0:D] + ident[:, D:P]], axis=1),
        "c_mask": mask,
    }


def build(nc, x, tok_w, w_qkv, b_rows, bv, beta, rw, rb, w1_d, w2_h, b2,
          c_pos, c_row, c_col, c_ident, c_mask, out):
    GW = (2 * NT - 1) * P
    WQ, WK, WV, WR = (slice(0, 2 * D), slice(2 * D, 4 * D), slice(4 * D, 5 * D), slice(5 * D, 5 * D + E))
    WC = 5 * D + E

    def by_slot(table, kinds):
        found = {}
        for g, slots_of in enumerate(table):
            for j, at in zip(kinds, slots_of):
                found.setdefault(at, []).append((g, j))
        return found

    stages = by_slot(STAGE_SLOTS, range(9))
    act_stages, dve_stages = by_slot(ACT_SLOTS, ACT_STAGES), by_slot(DVE_SLOTS, DVE_STAGES)
    choices = by_slot(CHOOSE_SLOTS, range(4))
    end_slot = max(max(stages), max(act_stages), max(dve_stages), max(choices)) + 1
    slots = range(-LAG, end_slot)
    group_of = {t // 2: g for g, (t0, n) in enumerate(GROUPS) for t in range(t0, t0 + n, 2)}
    late_q, late_v = ({LATE_QV[j] - LAG: 2, LATE_QV[j + 1] - LAG: 3} for j in (0, 2))
    NPAIR = NT // 2
    TAIL = len(GROUPS) - 1

    with ExitStack() as ctx:
        def sb(name, shape, dt=F32):
            return ctx.enter_context(nc.sbuf_tensor(name, shape, dt))

        def ps(name, shape):
            return ctx.enter_context(nc.psum_tensor(name, shape, F32))

        def sem(name):
            return ctx.enter_context(nc.semaphore(name))

        idx = sb("idx", [P, NT], I32)
        pos = sb("pos_or_res", [P, NT, D])
        res = pos
        ident_rev = sb("ident_rev", [P, P + E + D])
        ident, rev = ident_rev[:, 0:P], ident_rev[:, P:P + E]
        halves = ident_rev[:, P + E:P + E + D]
        NF = 16
        by_row = sb("by_row", [NF, P + 3])
        beta_all = sb("beta_all", [NF, 2])
        beta_sel = sb("beta_sel", [NF, 2])
        beta_col = sb("beta_col", [NF, 1])
        row_beta = sb("row_beta", [NF, P])
        row_hi = sb("row_hi", [NF, P])
        row_part = sb("row_part", [NF, P], F32R)
        col_or_hid = sb("col_or_hid", [P, (NB + 4) * CH * P])
        col_in = col_or_hid[0:NF, 0:GW]
        hid = col_or_hid[:, 0:NB * CH * P].rearrange("p (b s) -> p b s", b=NB)
        res_t = col_or_hid[:, NB * CH * P:(NB + 2) * CH * P].rearrange("p (g s) -> p g s", g=2)
        col_or_prt = sb("col_or_prt", [P, 8 * 512], F32R)
        col_part = col_or_prt[0:NF, 0:GW]
        prt = col_or_prt[:, :].rearrange("p (r b s) -> p r b s", r=2, b=4)
        prt_hi, prt_lo = prt[:, 0, :, :], prt[:, 1, :, :]
        bias = sb("bias", [P, GW])
        h0 = sb("h0", [P, NT, D])
        stats1 = sb("stats1", [P, NT, 6])
        mv1 = sb("mv1", [P, NT, 2])
        std1 = sb("std1", [P, NT])
        warm = sb("warm", [P, 1])
        var1 = sb("var1", [P, NT])
        near1 = sb("near1", [P, NT])
        nr = sb("nr", [P, 2, CH])
        rs_late = sb("rs_late", [P, 5, 2])
        std2 = sb("std2", [P, 2])
        rstd1 = sb("rstd1", [P, NT])
        shift1 = sb("shift1", [P, NT])
        xn1 = sb("xn1", [P, NT, D])
        x_or_hid = sb("x_or_hid", [P, 2 * S], F32R)
        xn1_split = x_or_hid[:, 0:S].rearrange("p (t d) -> p t d", t=NT)
        xt = x_or_hid[:, S:2 * S]
        hid_part = x_or_hid[:, :].rearrange("p (b r s) -> p b r s", b=NB, r=2)
        w_nat = sb("w_nat", [D, 3 * 2 * D])
        w_t = sb("w_t", [P, WC])
        w_hi = sb("w_hi", [P, WC], F32R)
        w_lo = sb("w_lo", [P, WC], F32R)
        b_nat = sb("b_nat", [2 + NB, P])
        b_col = sb("b_col", [P, 2 + NB])
        bv_all = sb("bv_all", [P, D])
        q_split = sb("q_split", [P, S], F32R)
        k_hi = sb("k_hi", [P, S], F32R)
        k_lo = sb("k_lo", [P, S], F32R)
        v = sb("v", [P, NT, D])
        v_split = sb("v_split", [P, NT, 2 * D], F32R)
        sc = sb("sc", [P, 2, S])
        pmax = sb("pmax", [P, NT, 4])
        pmax2 = sb("pmax2", [P, 2])
        nmax = sb("nmax", [P, NT])
        pr = sb("pr", [P, 4, S])
        psumh = sb("psumh", [P, NT, 2])
        den = sb("den", [P, NT])
        rden = sb("rden", [P, NT])
        ot = sb("ot", [P, 2 * P])
        h1 = sb("h1", [P, NT, D])
        stats2 = sb("stats2", [P, NT, 6])
        mv2 = sb("mv2", [P, NT, 2])
        rs2 = sb("rs2", [P, 5, 2])
        rstd2 = sb("rstd2", [P, NT])
        shift2 = sb("shift2", [P, 2])
        xn2 = sb("xn2", [P, CH, D])
        xn2_split = sb("xn2_split", [P, CH, 2 * D], F32R)
        x2t = sb("x2t", [P, 2, CH * P], F32R)
        rw_nat = sb("rw_nat", [E, 2 * D])
        rb_all = sb("rb_all", [P, E])
        logit = sb("logit", [P, CH, E])
        lmax = sb("lmax", [P, CH])
        tie = sb("tie", [P, CH, E])
        tmax = sb("tmax", [P, CH])
        chosen = sb("chosen", [P, CH, E])
        chosen_t = sb("chosen_t", [E, 2, CH * P], F32R)
        mask_f = sb("mask_f", [E, E * H])
        mask = sb("mask", [E, E * H], F32R)
        w1_nat = sb("w1_nat", [P, E * H])
        w1_hi = sb("w1_hi", [P, E * H], F32R)
        w1_lo = sb("w1_lo", [P, E * H], F32R)
        w2_s = sb("w2_s", [P, NB, D])
        w2_split = sb("w2_split", [P, NB, 2 * D], F32R)
        b2_s = sb("b2_s", [E, D])
        b2_split = sb("b2_split", [E, 2 * D], F32R)

        ps_s = ps("ps_s", [P, NB_S, 512])
        ps_t = ps("ps_t", [P, NB_T, 512])
        ps_o = ps("ps_o", [P, 512])
        ps_f = ps("ps_f", [P, NB_F, 512])

        idx_in, pos_in, const_in = sem("idx_in"), sem("pos_in"), sem("const_in")
        biasf_in, wqkv_in, wexp_in = sem("biasf_in"), sem("wqkv_in"), sem("wexp_in")
        tok_in = [sem(f"tok_in{c}") for c in range(NC)]
        pos_rest_in, bv_in, col_in_sem, out_sent = sem("pos_rest_in"), sem("bv_in"), sem("col_in_sem"), sem("out_sent")
        row_ready, biasmm, bias_act, bias_dve = sem("row_ready"), sem("biasmm"), sem("bias_act"), sem("bias_dve")
        wt_turned, wt_ready = sem("wt_turned"), sem("wt_ready")
        col_ready, v_copied, wt_step = sem("col_ready"), sem("v_copied"), sem("wt_step")
        stat_step, rs_step = sem("stat_step"), sem("rs_step")
        var1_ready, std1_ready, rstd1_ready = sem("var1_ready"), sem("std1_ready"), sem("rstd1_ready")
        xn1_hi_ready, xn1_ready, xt_turned, xt_ready = (
            sem("xn1_hi_ready"), sem("xn1_ready"), sem("xt_turned"), sem("xt_ready"))
        q_mm, k_mm, v_mm = sem("q_mm"), sem("k_mm"), sem("v_mm")
        q_hi_done, k_hi_done, q_ready, k_ready, v_ready = (
            sem("q_hi_done"), sem("k_hi_done"), sem("q_ready"), sem("k_ready"), sem("v_ready"))
        expw_ready = sem("expw_ready")
        s_mm = sem("s_mm")
        s_read = sem("s_read")
        pmax2_done, nmax_ready = sem("pmax2_done"), sem("nmax_ready")
        exp_done = sem("exp_done")
        p_turned = sem("p_turned")
        p_hi = sem("p_hi")
        p_lo = sem("p_lo")
        pv_mm = sem("pv_mm")
        ot_ready = sem("ot_ready")
        ot_turned = sem("ot_turned")
        den_done, rden_done, stats2_done = sem("den_done"), sem("rden_done"), sem("stats2_done")
        h1_done = sem("h1_done")
        var2_ready, std2_ready, rstd2_ready = sem("var2_ready"), sem("std2_ready"), sem("rstd2_ready")
        xn2_hi_ready, late_xs_ready = sem("xn2_hi_ready"), sem("late_xs_ready")
        mv2_ready, xs_ready = sem("mv2_ready"), sem("xs_ready")
        x2_turned, x2t_ready = sem("x2_turned"), sem("x2t_ready")
        logit_mm, chosen_ready, chosen_turned = sem("logit_mm"), sem("chosen_ready"), sem("chosen_turned")
        chosen_t_ready = sem("chosen_t_ready")
        hid_mm, hid_ready, hid_lo_ready = sem("hid_mm"), sem("hid_ready"), sem("hid_lo_ready")
        out_mm, res_t_ready, out_turned, res_done = sem("out_mm"), sem("res_t_ready"), sem("out_turned"), sem("res_done")
        logit_read, choose_step = sem("logit_read"), sem("choose_step")
        dve_step, pool_step, act_step = sem("dve_step"), sem("pool_step"), sem("act_step")

        block = ctx.enter_context(nc.Block())

        BW = [min(512, GW - 512 * j) for j in range(-(-GW // 512))]
        half = S // 2

        s_free, t_free = 4 * NT - LAG + 2, 4 * NT + 3
        stage_bank, turn = {}, 0
        for k in slots:
            m, at = (k - OUT_LAG) // 8, (k - OUT_LAG) % 8
            for use in ([("out", m)] if at == 0 and 0 <= m < NPAIR else []) + stages.get(k, []):
                banks = ["f0", "f1"] + ["s0", "s1"] * (k >= s_free) + ["t0", "t1", "t2"] * (k >= t_free)
                stage_bank[use] = banks[turn % len(banks)]
                turn += 1
        bank_of = {}
        for name, bank, n in (("f", ps_f, NB_F), ("s", ps_s, NB_S), ("t", ps_t, NB_T)):
            for b in range(n):
                bank_of[f"{name}{b}"] = bank[:, b, :]
        bias_bank = [ps_s[:, 0, :], ps_s[:, 1, :], ps_f[:, 1, :]]

        def q_bank(c):
            return ps_t[:, 2, :] if c % 2 else ps_o[:, :]

        def hid_cols(g):
            w = GROUPS[g][1] * P
            return slice(w, 2 * w) if g == TAIL else slice(0, w)

        def f_bank(g, j):
            return bank_of[stage_bank[g, j]]

        @block.sync
        def _(sp):
            sp.dma_start(idx[:, :], x.rearrange("a (p i) -> (a p) i", p=P)).then_inc(idx_in, 16)
            sp.dma_start(by_row[:, :], c_row).then_inc(biasf_in, 16)
            sp.dma_start(beta_all[:, :], beta.partition_broadcast(NF)).then_inc(biasf_in, 16)
            sp.dma_start(b_nat[:, :], b_rows).then_inc(wqkv_in, 16)
            pos_v = c_pos.rearrange("p (i d) -> p i d", d=D)
            sp.dma_start(pos[:, 0:CH, :], pos_v[:, 0:CH, :]).then_inc(pos_in, 16)
            sp.dma_start(pos[:, CH:NT, :], pos_v[:, CH:NT, :]).then_inc(pos_rest_in, 16)
            sp.dma_start(bv_all[:, :], bv.partition_broadcast(P)).then_inc(bv_in, 16)
            sp.wait_ge(tok_in[NC - 2], CH * 16)
            sp.dma_start(w1_nat[:, :], w1_d).then_inc(wexp_in, 16)
            sp.dma_start(mask_f[:, :], c_mask).then_inc(wexp_in, 16)
            sp.dma_start(w2_s[:, :, :], w2_h.rearrange("p (b d) -> p b d", b=NB)).then_inc(wexp_in, 16)
            sp.dma_start(b2_s[:, :], b2).then_inc(wexp_in, 16)
            sp.dma_start(rb_all[:, :], rb.partition_broadcast(P)).then_inc(wexp_in, 16)
            out_v = out.rearrange("a (p i) d -> (a p) i d", p=P)
            for g, (t0, n) in enumerate(GROUPS):
                sp.wait_ge(res_done, g + 1)
                sp.dma_start(out_v[:, t0:t0 + n, :], res[:, t0:t0 + n, :]).then_inc(out_sent, 16)
            sp.wait_ge(out_sent, 16 * len(GROUPS))

        @block.gpsimd
        def _(pool):
            nc.gpsimd.dma_start(col_part[:, :], c_col).then_inc(col_in_sem, 16)
            pool.wait_ge(idx_in, 16)
            for i in range(NT):
                nc.gpsimd.indirect_dma_start(
                    out=h0[:, i, :], out_offset=None, in_=tok_w,
                    in_offset=bass.IndirectOffsetOnAxis(ap=idx[:, i:i + 1], axis=0),
                ).then_inc(tok_in[i // CH], 16)
            own = [0]

            def then_own(ins):
                ins.then_inc(pool_step, 1)
                own[0] += 1
                pool.wait_ge(pool_step, own[0])

            pool.wait_ge(bv_in, 16)
            for c in range(NC):
                tiles = slice(CH * c, CH * (c + 1))
                pool.wait_ge(v_copied, c + 1)
                then_own(nc.gpsimd.tensor_tensor(v[:, tiles, :], v[:, tiles, :],
                                                 bv_all[:, :].unsqueeze(1).to_broadcast([P, CH, D]), ALU.add))
                then_own(nc.gpsimd.tensor_copy(v_split[:, tiles, 0:D], v[:, tiles, :]))
                nc.gpsimd.tensor_tensor(v_split[:, tiles, D:2 * D], v[:, tiles, :],
                                        v_split[:, tiles, 0:D].bitcast(F32), ALU.subtract).then_inc(v_ready, 1)
            pool.wait_ge(wexp_in, 5 * 16)
            w1_f = w1_nat[:, :]
            nc.gpsimd.tensor_copy(w1_hi[:, :], w1_f)
            nc.gpsimd.tensor_copy(mask[:, :], mask_f[:, :])
            nc.gpsimd.tensor_copy(w2_split[:, :, 0:D], w2_s[:, :, :])
            then_own(nc.gpsimd.tensor_copy(b2_split[:, 0:D], b2_s[:, :]))
            nc.gpsimd.tensor_tensor(w1_lo[:, :], w1_f, w1_hi[:, :].bitcast(F32), ALU.subtract)
            nc.gpsimd.tensor_tensor(w2_split[:, :, D:2 * D], w2_s[:, :, :], w2_split[:, :, 0:D].bitcast(F32), ALU.subtract)
            nc.gpsimd.tensor_tensor(b2_split[:, D:2 * D], b2_s[:, :], b2_split[:, 0:D].bitcast(F32), ALU.subtract
                                    ).then_inc(expw_ready, 1)

            def hidden_lo(g):
                for b in range(NB):
                    pool.wait_ge(hid_ready, NB * g + b + 1)
                    w = GROUPS[g][1] * P
                    nc.gpsimd.tensor_tensor(hid_part[:, b, 1, 0:w], hid[:, b, 0:w], hid_part[:, b, 0, 0:w].bitcast(F32),
                                            ALU.subtract).then_inc(hid_lo_ready, 1)

            for m in range(NPAIR):
                if m == POOL_HIDDEN[0]:
                    hidden_lo(0)
                if m == POOL_HIDDEN[1]:
                    hidden_lo(1)
                if m == LATE:
                    break
                g = group_of[m]
                tiles = slice(2 * m, 2 * m + 2)
                here = slice(2 * m % CH, 2 * m % CH + 2)
                pool.wait_ge(mv2_ready, m + 1)
                if m >= 2:
                    pool.wait_ge(x2_turned, group_of[m - 2] + 1)
                v2, h2, y, t, u = (rs2[:, r, :] for r in range(5))
                then_own(nc.gpsimd.tensor_scalar(v2, mv2[:, tiles, 1], EPS, None, ALU.add))
                nc.gpsimd.tensor_scalar(h2, v2, -0.5, None, ALU.mult)
                then_own(nc.gpsimd.tensor_scalar(y.bitcast(I32), v2.bitcast(I32), -0.5, RSQRT_MAGIC, ALU.mult, ALU.add))
                for step in range(3):
                    then_own(nc.gpsimd.tensor_tensor(t, y, y, ALU.mult))
                    then_own(nc.gpsimd.tensor_tensor(u, t, h2, ALU.mult))
                    then_own(nc.gpsimd.tensor_scalar(t, u, 1.5, None, ALU.add))
                    then_own(nc.gpsimd.tensor_tensor(rstd2[:, tiles] if step == 2 else y, t, y, ALU.mult))
                for t in range(2):
                    ins = nc.gpsimd.tensor_scalar(xn2[:, here, :][:, t, :], h1[:, 2 * m + t, :], mv2[:, 2 * m + t, 0:1],
                                                  rstd2[:, 2 * m + t:2 * m + t + 1], ALU.subtract, ALU.mult)
                then_own(ins)
                then_own(nc.gpsimd.tensor_copy(xn2_split[:, here, 0:D], xn2[:, here, :]))
                nc.gpsimd.tensor_tensor(xn2_split[:, here, D:2 * D], xn2[:, here, :],
                                        xn2_split[:, here, 0:D].bitcast(F32), ALU.subtract).then_inc(xs_ready, 1)

        @block.scalar
        def _(act):
            act.dma_start(w_nat[:, :], w_qkv).then_inc(wqkv_in, 16)
            act.dma_start(ident_rev[:, :], c_ident).then_inc(const_in, 16)
            act.dma_start(rw_nat[:, :], rw).then_inc(wqkv_in, 16)
            act.wait_ge(const_in, 16)
            nc.scalar.activation(warm[:, :], rev[:, 0:1], ACT.Sqrt)

            def bias_piece(j):
                act.wait_ge(biasmm, j + 1)
                nc.scalar.activation(bias[:, 512 * j:512 * j + BW[j]], bias_bank[j % 3][:, 0:BW[j]], ACT.Copy
                                     ).then_inc(bias_act, 1)

            def std(c):
                tiles = slice(CH * c, CH * (c + 1))
                act.wait_ge(var1_ready, c + 1)
                nc.scalar.activation(std1[:, tiles], var1[:, tiles], ACT.Sqrt).then_inc(std1_ready, 1)

            def normalise(c):
                act.wait_ge(rstd1_ready, c + 1)
                for t in range(CH * c, CH * (c + 1)):
                    ins = nc.scalar.activation(xn1[:, t, :], h0[:, t, :], ACT.Identity, bias=shift1[:, t:t + 1],
                                               scale=rstd1[:, t:t + 1])
                ins.then_inc(act_step, 1)

            def x_hi(c):
                tiles = slice(CH * c, CH * (c + 1))
                act.wait_ge(act_step, c + 1)
                nc.scalar.activation(xn1_split[:, tiles, 0:D], xn1[:, tiles, :], ACT.Copy).then_inc(xn1_hi_ready, 1)

            def copy_xt(c):
                act.wait_ge(xt_turned, c + 1)
                nc.scalar.activation(xt[:, c * 512:(c + 1) * 512], ps_t[:, 0, :], ACT.Copy).then_inc(xt_ready, 1)

            def copy_k(c):
                act.wait_ge(k_mm, c + 1)
                nc.scalar.activation(k_hi[:, c * 512:(c + 1) * 512], ps_f[:, 0, :], ACT.Identity, bias=b_col[:, 1:2]
                                     ).then_inc(k_hi_done, 1)

            def copy_q(c):
                act.wait_ge(q_mm, c + 1)
                nc.scalar.activation(q_split[:, c * 512:(c + 1) * 512], q_bank(c), ACT.Identity, bias=b_col[:, 0:1]
                                     ).then_inc(q_hi_done, 1)

            def copy_v(c):
                act.wait_ge(v_mm, c + 1)
                nc.scalar.activation(v[:, CH * c:CH * (c + 1), :], ps_t[:, 1, 0:CH * D].rearrange("p (t d) -> p t d", d=D),
                                     ACT.Copy).then_inc(v_copied, 1)

            def load_exp():
                nc.scalar.activation(warm[:, :], rev[:, 0:1], ACT.Exp)

            std(0)
            bias_piece(1)
            normalise(0)
            x_hi(0)
            std(1)
            normalise(1)
            copy_xt(0)
            x_hi(1)
            bias_piece(3)
            std(2)
            copy_k(0)
            copy_q(0)
            normalise(2)
            copy_xt(1)
            std(3)
            x_hi(2)
            copy_k(1)
            bias_piece(5)
            bias_piece(7)
            copy_xt(2)
            normalise(3)
            x_hi(3)
            copy_k(2)
            copy_xt(3)
            copy_q(1)
            load_exp()
            copy_v(0)
            copy_k(3)
            copy_v(1)

            def exp_half(t, a):
                m = t // 2
                if a == 0:
                    act.wait_ge(nmax_ready, t + 1)
                if m >= 2:
                    act.wait_ge(p_turned, 8 * (m - 2) + 4 * (a + 1))
                cols = slice(a * half, (a + 1) * half)
                nc.scalar.activation(pr[:, t % 4, cols], sc[:, t % 2, cols], ACT.Exp, bias=nmax[:, t:t + 1],
                                     accum_out=psumh[:, t, a:a + 1]).then_inc(exp_done, 1)

            def copy_hi(k):
                act.wait_ge(p_turned, k + 1)
                if k >= 4:
                    act.wait_ge(pv_mm, k - 3)
                nc.scalar.activation(prt_hi[:, k % 4, :], ps_t[:, k % NB_T, :], ACT.Copy).then_inc(p_hi, 1)

            def copy_out(m):
                act.wait_ge(pv_mm, 8 * (m + 1))
                if m >= 1:
                    act.wait_ge(ot_turned, m)
                nc.scalar.activation(ot[:, :], ps_o[:, 0:2 * P], ACT.Copy).then_inc(ot_ready, 1)

            def expert(g, j):
                t0, n = GROUPS[g]
                w = n * P
                cols = hid_cols(g)
                bank = f_bank(g, j)
                if j == 0:
                    act.wait_ge(x2_turned, g + 1)
                    if g >= 2:
                        act.wait_ge(hid_mm, NB * (g - 1))
                    nc.scalar.activation(x2t[:, g % 2, 0:w], bank[:, 0:w], ACT.Copy).then_inc(x2t_ready, 1)
                elif j == 2:
                    act.wait_ge(chosen_turned, g + 1)
                    if g >= 2:
                        act.wait_ge(out_mm, g - 1)
                    nc.scalar.activation(chosen_t[:, g % 2, 0:w], bank[0:E, 0:w], ACT.Copy).then_inc(chosen_t_ready, 1)
                elif 3 <= j <= 6:
                    b = j - 3
                    act.wait_ge(hid_mm, NB * g + b + 1)
                    if g >= 1:
                        act.wait_ge(out_mm, g if g < TAIL else g - 1)
                        act.wait_ge(hid_lo_ready, NB * (g - 1) + b + 1)
                    ins = nc.scalar.activation(hid[:, b, 0:w], bank[:, 0:w], ACT.Relu, bias=b_col[:, 2 + b:3 + b])
                    if g < LATE_HID:
                        ins = nc.scalar.activation(hid_part[:, b, 0, cols], bank[:, 0:w], ACT.Relu,
                                                   bias=b_col[:, 2 + b:3 + b])
                    ins.then_inc(hid_ready, 1)
                elif j == 7:
                    act.wait_ge(out_mm, g + 1)
                    nc.scalar.activation(res_t[:, g % 2, 0:w], bank[:, 0:w], ACT.Copy).then_inc(res_t_ready, 1)

            def late_std(i):
                act.wait_ge(var2_ready, i + 1)
                nc.scalar.activation(std2[:, :], rs_late[:, 0, :], ACT.Sqrt).then_inc(std2_ready, 1)

            def late_normalise(i):
                m = LATE + i
                here = slice(2 * m % CH, 2 * m % CH + 2)
                act.wait_ge(rstd2_ready, i + 1)
                act.wait_ge(x2_turned, group_of[m - 2] + 1)
                for t in range(2):
                    ins = nc.scalar.activation(xn2[:, here, :][:, t, :], h1[:, 2 * m + t, :], ACT.Identity,
                                               bias=shift2[:, t:t + 1], scale=rstd2[:, 2 * m + t:2 * m + t + 1])
                ins.then_inc(act_step, 1)
                act.wait_ge(act_step, NC + i + 1)
                nc.scalar.activation(xn2_split[:, here, 0:D], xn2[:, here, :], ACT.Copy).then_inc(xn2_hi_ready, 1)

            for k in slots:
                if k in late_v:
                    copy_v(late_v[k])
                if k in late_q:
                    copy_q(late_q[k])
                m, at = (k - COPY_OUT_AT) // 8, (k - COPY_OUT_AT) % 8
                if at == 0 and 0 <= m < NPAIR:
                    copy_out(m)
                for g, j in act_stages.get(k, []):
                    expert(g, j)
                for i, (var_at, rs_at, _) in enumerate(LATE_SLOTS):
                    if k == var_at:
                        late_std(i)
                    if k == rs_at:
                        late_normalise(i)
                if 0 <= k < 4 * NT:
                    copy_hi(k)
                for e in range(4):
                    m, at = (k + LAG - EXP_AT[e]) // 8, (k + LAG - EXP_AT[e]) % 8
                    if at == 0 and 0 <= m < NPAIR:
                        exp_half(2 * m + e // 2, e % 2)

        @block.tensor
        def _(pe):
            pe.wait_ge(const_in, 16)
            pe.wait_ge(wqkv_in, 3 * 16)
            for r in range(3):
                nc.tensor.transpose(ps_t[:, 0, r * D:(r + 1) * D], w_nat[:, 2 * D * r:2 * D * (r + 1)], ident[0:D, 0:D])
            nc.tensor.transpose(ps_t[:, 0, 3 * D:3 * D + E], rw_nat[:, :], ident[0:E, 0:E])
            nc.tensor.transpose(ps_t[:, 0, 3 * D + E:3 * D + E + 2 + NB], b_nat[:, :], ident[0:2 + NB, 0:2 + NB]
                                ).then_inc(wt_turned, 1)
            pe.wait_ge(row_ready, 1)
            pe.wait_ge(col_in_sem, 16)

            def bias_piece(j):
                if j >= 3:
                    i = j - 3
                    pe.wait_ge(bias_act if i % 2 else bias_dve, i // 2 + 1)
                nc.tensor.matmul(bias_bank[j % 3][:, 0:BW[j]], row_part[:, :],
                                 col_part[:, 512 * j:512 * j + BW[j]], start=True, stop=True).then_inc(biasmm, 1)

            def turn_x(c):
                pe.wait_ge(xn1_ready, c + 1)
                if c == 0:
                    pe.wait_ge(wt_ready, 1)
                else:
                    pe.wait_ge(xt_ready, c)
                for t in range(CH):
                    mm = nc.tensor.transpose(ps_t[:, 0, t * P:(t + 1) * P],
                                             xn1_split[:, CH * c + t, :].bitcast(F32), ident)
                mm.then_inc(xt_turned, 1)

            def make_k(c):
                cols = slice(c * 512, (c + 1) * 512)
                pe.wait_ge(xt_ready, c + 1)
                if c >= 1:
                    pe.wait_ge(k_ready, c)
                nc.tensor.matmul(ps_f[:, 0, :], w_hi[:, WK], xt[:, cols], start=True, stop=False)
                nc.tensor.matmul(ps_f[:, 0, :], w_lo[:, WK], xt[:, cols], start=False, stop=True).then_inc(k_mm, 1)

            def make_q(c):
                cols = slice(c * 512, (c + 1) * 512)
                pe.wait_ge(xt_ready, c + 1)
                if c >= 2:
                    pe.wait_ge(q_ready, c - 1)
                nc.tensor.matmul(q_bank(c), w_hi[:, WQ], xt[:, cols], start=True, stop=False)
                nc.tensor.matmul(q_bank(c), w_lo[:, WQ], xt[:, cols], start=False, stop=True).then_inc(q_mm, 1)

            def make_v(c):
                pe.wait_ge(xt_ready, c + 1)
                if c >= 1:
                    pe.wait_ge(v_copied, c)
                for t in range(CH):
                    x_t = xt[:, (CH * c + t) * P:(CH * c + t + 1) * P]
                    o = ps_t[:, 1, t * D:(t + 1) * D]
                    nc.tensor.matmul(o, x_t, w_hi[:, WV], start=True, stop=False)
                    mm = nc.tensor.matmul(o, x_t, w_lo[:, WV], start=False, stop=True)
                mm.then_inc(v_mm, 1)

            def scores(u):
                t, b = u // 4, u % 4
                if u == 0:
                    pe.wait_ge(q_ready, 1)
                    pe.wait_ge(bias_act, len(BW) // 2)
                    pe.wait_ge(bias_dve, (len(BW) + 1) // 2)
                if t == 0:
                    pe.wait_ge(k_ready, b + 1)
                if t > 0 and t % CH == 0 and b == 0:
                    pe.wait_ge(q_ready, t // CH + 1)
                if u >= NB_S:
                    pe.wait_ge(s_read, u - NB_S + 1)
                queries = q_split[:, t * P:(t + 1) * P]
                keys = slice(b * 512, (b + 1) * 512)
                nc.tensor.matmul(ps_s[:, u % NB_S, :], queries, k_hi[:, keys], start=True, stop=False)
                nc.tensor.matmul(ps_s[:, u % NB_S, :], queries, k_lo[:, keys], start=False, stop=True).then_inc(s_mm, 1)

            def turn(k):
                m, q = k // 8, k % 8
                if q % 4 == 0:
                    pe.wait_ge(exp_done, 4 * m + 3 + q // 4)
                if k >= NB_T:
                    pe.wait_ge(p_lo, k - NB_T + 1)
                if k == 0:
                    pe.wait_ge(v_copied, NC)
                    pe.wait_ge(q_ready, NC)
                for b in range(2):
                    for t in range(2):
                        mm = nc.tensor.transpose(ps_t[:, k % NB_T, (2 * b + t) * P:(2 * b + t + 1) * P],
                                                 pr[:, (2 * m + t) % 4, (2 * q + b) * P:(2 * q + b + 1) * P], ident)
                mm.then_inc(p_turned, 1)

            def times_v(k):
                m, q = k // 8, k % 8
                pe.wait_ge(p_lo, k + 1)
                if k == 0:
                    pe.wait_ge(v_ready, NC)
                if q == 0 and m >= 1:
                    pe.wait_ge(ot_ready, m)
                for b in range(2):
                    cols, values = slice(2 * b * P, 2 * (b + 1) * P), v_split[:, 2 * q + b, :]
                    nc.tensor.matmul(ps_o[:, 0:2 * P], values, prt_hi[:, k % 4, cols],
                                     start=(q == 0 and b == 0), stop=False)
                    mm = nc.tensor.matmul(ps_o[:, 0:2 * P], values, prt_lo[:, k % 4, cols],
                                          start=False, stop=(q == 7 and b == 1))
                mm.then_inc(pv_mm, 1)

            last_read = {"f0": (k_ready, NC), "f1": (bias_dve, (len(BW) + 1) // 2)}
            last_read.update({f"s{b}": (s_read, 4 * NT) for b in range(NB_S)})
            last_read.update({f"t{b}": (p_lo, 4 * NT) for b in range(NB_T)})

            def turn_out(m):
                pe.wait_ge(ot_ready, m + 1)
                bank = stage_bank["out", m]
                pe.wait_ge(*last_read[bank])
                for t in range(2):
                    mm = nc.tensor.matmul(bank_of[bank][:, t * D:(t + 1) * D], ot[:, t * P:(t + 1) * P], halves,
                                          start=True, stop=True)
                mm.then_inc(ot_turned, 1)
                last_read[bank] = (h1_done, m + 1)

            def expert(g, j):
                t0, n = GROUPS[g]
                w = n * P
                cols = hid_cols(g)
                bank = f_bank(g, j)
                x_all = x2t[:, g % 2, :]
                pe.wait_ge(*last_read[stage_bank[g, j]])
                if j == 0:
                    if t0 // 2 < LATE:
                        pe.wait_ge(xs_ready, (t0 + n) // 2)
                    else:
                        pe.wait_ge(late_xs_ready, (t0 + n) // 2 - LATE)
                    for t in range(n):
                        mm = nc.tensor.transpose(bank[:, t * P:(t + 1) * P], xn2_split[:, (t0 + t) % CH, :].bitcast(F32), ident)
                    mm.then_inc(x2_turned, 1)
                    last_read[stage_bank[g, j]] = (x2t_ready, g + 1)
                elif j == 1:
                    pe.wait_ge(x2t_ready, g + 1)
                    if g == 0:
                        pe.wait_ge(expw_ready, 1)
                    for t in range(n):
                        x_t = x_all[:, t * P:(t + 1) * P]
                        nc.tensor.matmul(bank[:, t * E:(t + 1) * E], x_t, w_hi[:, WR], start=True, stop=False)
                        mm = nc.tensor.matmul(bank[:, t * E:(t + 1) * E], x_t, w_lo[:, WR], start=False, stop=True)
                    mm.then_inc(logit_mm, 1)
                    last_read[stage_bank[g, j]] = (logit_read, g + 1)
                elif j == 2:
                    pe.wait_ge(chosen_ready, g + 1)
                    for t in range(n):
                        mm = nc.tensor.transpose(bank[0:E, t * P:(t + 1) * P], chosen[:, t, :], ident)
                    mm.then_inc(chosen_turned, 1)
                    last_read[stage_bank[g, j]] = (chosen_t_ready, g + 1)
                elif j <= 6:
                    b = j - 3
                    if b == 0:
                        pe.wait_ge(chosen_t_ready, g + 1)
                    rows = slice(b * P, (b + 1) * P)
                    nc.tensor.matmul(bank[:, 0:w], w1_hi[:, rows], x_all[:, 0:w], start=True, stop=False)
                    nc.tensor.matmul(bank[:, 0:w], w1_lo[:, rows], x_all[:, 0:w], start=False, stop=False)
                    nc.tensor.matmul(bank[:, 0:w], mask[:, rows], chosen_t[:, g % 2, 0:w],
                                     start=False, stop=True).then_inc(hid_mm, 1)
                    last_read[stage_bank[g, j]] = (hid_ready, NB * g + b + 1)
                elif j == 7:
                    nc.tensor.matmul(bank[:, 0:w], b2_split[:, :], chosen_t[:, g % 2, 0:w], start=True, stop=False)
                    for b in range(NB):
                        pe.wait_ge(hid_lo_ready, NB * g + b + 1)
                        nc.tensor.matmul(bank[:, 0:w], w2_split[:, b, :], hid_part[:, b, 0, cols], start=False, stop=False)
                        mm = nc.tensor.matmul(bank[:, 0:w], w2_split[:, b, :], hid_part[:, b, 1, cols],
                                              start=False, stop=(b == NB - 1))
                    mm.then_inc(out_mm, 1)
                    last_read[stage_bank[g, j]] = (res_t_ready, g + 1)
                else:
                    pe.wait_ge(res_t_ready, g + 1)
                    for t in range(n):
                        mm = nc.tensor.matmul(bank[:, t * D:(t + 1) * D], res_t[:, g % 2, t * P:(t + 1) * P], halves,
                                              start=True, stop=True)
                    mm.then_inc(out_turned, 1)
                    last_read[stage_bank[g, j]] = (res_done, g + 1)

            for j in range(5):
                bias_piece(j)
            bias_piece(5)
            turn_x(0)
            make_k(0)
            make_q(0)
            turn_x(1)
            bias_piece(6)
            bias_piece(7)
            make_k(1)
            turn_x(2)
            scores(0)
            make_k(2)
            scores(1)
            turn_x(3)
            make_q(1)
            make_v(0)
            make_k(3)
            scores(2)
            make_v(1)

            for k in slots:
                if k in late_v:
                    make_v(late_v[k])
                if k in late_q:
                    make_q(late_q[k])
                m, at = (k - OUT_LAG) // 8, (k - OUT_LAG) % 8
                if at == 0 and 0 <= m < NPAIR:
                    turn_out(m)
                for g, j in stages.get(k, []):
                    expert(g, j)
                if 0 <= k < 4 * NT:
                    turn(k)
                if EARLY <= k + LAG < 4 * NT:
                    scores(k + LAG)
                if 3 <= k < 4 * NT + 3:
                    times_v(k - 3)

        @block.vector
        def _(dve):
            steps = [0]

            def then_own(ins):
                ins.then_inc(dve_step, 1)
                steps[0] += 1
                dve.wait_ge(dve_step, steps[0])

            def newton_1(t, near, var):
                return nc.vector.tensor_tensor(t, near, var, ALU.mult)

            def newton_2(u, t, near):
                return nc.vector.scalar_tensor_tensor(u, t, -0.5, near, ALU.mult, ALU.mult)

            def newton_3(dst, u, near):
                return nc.vector.scalar_tensor_tensor(dst, u, 1.5, near, ALU.add, ALU.mult)

            dve.wait_ge(biasf_in, 2 * 16)
            then_own(nc.vector.tensor_tensor(beta_sel[:, :], beta_all[:, :], by_row[:, P + 1:P + 3], ALU.mult))
            then_own(nc.vector.tensor_reduce(beta_col[:, :], beta_sel[:, :], AX.X, ALU.add))
            then_own(nc.vector.tensor_scalar(row_beta[:, :], by_row[:, 0:P], beta_col[:, 0:1], None, ALU.mult))
            then_own(nc.vector.tensor_copy(row_part[:, :], row_beta[:, :]))
            then_own(nc.vector.tensor_scalar(row_hi[:, :], row_part[:, :].bitcast(F32), by_row[:, P:P + 1], None, ALU.mult))
            nc.vector.tensor_tensor(row_part[:, :], row_beta[:, :], row_hi[:, :], ALU.subtract).then_inc(row_ready, 1)

            def add_position(c):
                tiles = slice(CH * c, CH * (c + 1))
                if c <= 1:
                    dve.wait_ge(pos_rest_in if c else pos_in, 16)
                dve.wait_ge(tok_in[c], CH * 16)
                nc.vector.tensor_tensor(h0[:, tiles, :], h0[:, tiles, :], pos[:, tiles, :], ALU.add
                                        ).then_inc(stat_step, 1)

            def chunk_stats(c):
                dve.wait_ge(stat_step, 3 * c + 1)
                for t in range(CH * c, CH * (c + 1)):
                    st = nc.vector.bn_stats(stats1[:, t, :], h0[:, t, :])
                st.then_inc(stat_step, 1)

            def chunk_moments(c):
                dve.wait_ge(stat_step, 3 * c + 2)
                for t in range(CH * c, CH * (c + 1)):
                    st = nc.vector.bn_aggr(mv1[:, t, :], stats1[:, t, :])
                st.then_inc(stat_step, 1)

            def chunk_var(c):
                tiles = slice(CH * c, CH * (c + 1))
                dve.wait_ge(stat_step, 3 * c + 3)
                nc.vector.tensor_scalar(var1[:, tiles], mv1[:, tiles, 1], EPS, None, ALU.add).then_inc(var1_ready, 1)

            def chunk_reciprocal(c):
                tiles = slice(CH * c, CH * (c + 1))
                dve.wait_ge(std1_ready, c + 1)
                nc.vector.reciprocal(near1[:, tiles], std1[:, tiles]).then_inc(rs_step, 1)

            def chunk_newton(c):
                tiles = slice(CH * c, CH * (c + 1))
                dve.wait_ge(rs_step, c + 1)
                then_own(newton_1(nr[:, 0, 0:CH], near1[:, tiles], var1[:, tiles]))
                then_own(newton_2(nr[:, 1, 0:CH], nr[:, 0, 0:CH], near1[:, tiles]))
                then_own(newton_3(rstd1[:, tiles], nr[:, 1, 0:CH], near1[:, tiles]))
                nc.vector.scalar_tensor_tensor(shift1[:, tiles], mv1[:, tiles, 0], -1.0, rstd1[:, tiles],
                                               ALU.mult, ALU.mult).then_inc(rstd1_ready, 1)

            def x_lo(c):
                tiles = slice(CH * c, CH * (c + 1))
                dve.wait_ge(xn1_hi_ready, c + 1)
                nc.vector.tensor_tensor(xn1_split[:, tiles, D:2 * D], xn1[:, tiles, :],
                                        xn1_split[:, tiles, 0:D].bitcast(F32), ALU.subtract).then_inc(xn1_ready, 1)

            def split_k(c):
                cols = slice(c * 512, (c + 1) * 512)
                dve.wait_ge(k_hi_done, c + 1)
                nc.vector.scalar_tensor_tensor(k_lo[:, cols], ps_f[:, 0, :], b_col[:, 1:2], k_hi[:, cols].bitcast(F32),
                                               ALU.add, ALU.subtract).then_inc(k_ready, 1)

            def split_q(c):
                cols = slice(c * 512, (c + 1) * 512)
                dve.wait_ge(q_hi_done, c + 1)
                nc.vector.scalar_tensor_tensor(q_split[D:2 * D, cols], q_bank(c)[D:2 * D, :], b_col[D:2 * D, 0:1],
                                               q_split[D:2 * D, cols].bitcast(F32), ALU.add, ALU.subtract
                                               ).then_inc(q_ready, 1)

            def bias_piece(j):
                dve.wait_ge(biasmm, j + 1)
                nc.vector.tensor_copy(bias[:, 512 * j:512 * j + BW[j]], bias_bank[j % 3][:, 0:BW[j]]).then_inc(bias_dve, 1)

            def add_bias(u):
                t, b = u // 4, u % 4
                dve.wait_ge(s_mm, u + 1)
                if t >= 2:
                    dve.wait_ge(exp_done, 2 * (t - 2) + b // 2 + 1)
                b0 = (NT - 1 - t) * P + b * 512
                nc.vector.tensor_tensor_reduce(sc[:, t % 2, b * 512:(b + 1) * 512], ps_s[:, u % NB_S, :],
                                               bias[:, b0:b0 + 512], 1.0, -3.0e38, ALU.add, ALU.max,
                                               pmax[:, t, b:b + 1]).then_inc(s_read, 1)

            dve.wait_ge(wt_turned, 1)
            for r in range(2):
                nc.vector.tensor_scalar(w_t[:, 2 * D * r:2 * D * (r + 1)].rearrange("p (s e) -> p s e", s=2),
                                        ps_t[:, 0, r * D:(r + 1) * D].unsqueeze(1).to_broadcast([P, 2, D]),
                                        1.0 if r else D ** -0.5, None, ALU.mult)
            nc.vector.tensor_copy(w_t[:, 4 * D:WC], ps_t[:, 0, 2 * D:3 * D + E])
            nc.vector.tensor_scalar(b_col[:, 0:1], ps_t[:, 0, 3 * D + E:3 * D + E + 1], D ** -0.5, None, ALU.mult)
            nc.vector.tensor_copy(b_col[:, 1:2 + NB], ps_t[:, 0, 3 * D + E + 1:3 * D + E + 2 + NB]).then_inc(wt_step, 1)
            add_position(0)
            dve.wait_ge(wt_step, 1)
            nc.vector.tensor_copy(w_hi[:, :], w_t[:, :]).then_inc(wt_step, 1)
            chunk_stats(0)
            dve.wait_ge(wt_step, 2)
            nc.vector.tensor_tensor(w_lo[:, :], w_t[:, :], w_hi[:, :].bitcast(F32), ALU.subtract).then_inc(wt_ready, 1)
            chunk_moments(0)
            chunk_var(0)
            bias_piece(0)
            bias_piece(2)
            chunk_reciprocal(0)
            chunk_newton(0)
            add_position(1)
            chunk_stats(1)
            chunk_moments(1)
            chunk_var(1)
            chunk_reciprocal(1)
            x_lo(0)
            chunk_newton(1)
            add_position(2)
            bias_piece(4)
            chunk_stats(2)
            x_lo(1)
            chunk_moments(2)
            chunk_var(2)
            chunk_reciprocal(2)
            split_k(0)
            chunk_newton(2)
            split_q(0)
            add_position(3)
            chunk_stats(3)
            bias_piece(6)
            chunk_moments(3)
            chunk_var(3)
            chunk_reciprocal(3)
            x_lo(2)
            split_k(1)
            chunk_newton(3)
            x_lo(3)
            add_bias(0)
            split_k(2)
            split_q(1)
            add_bias(1)
            add_bias(2)
            split_k(3)

            def half_max(t):
                dve.wait_ge(s_read, 4 * t + 4)
                nc.vector.tensor_tensor(pmax2[:, :], pmax[:, t, 0:2], pmax[:, t, 2:4], ALU.max).then_inc(pmax2_done, 1)

            def row_max(t):
                dve.wait_ge(pmax2_done, t + 1)
                nc.vector.tensor_scalar(nmax[:, t:t + 1], pmax2[:, 0:1], pmax2[:, 1:2], -1.0,
                                        ALU.max, ALU.mult).then_inc(nmax_ready, 1)

            def copy_lo(k):
                dve.wait_ge(p_hi, k + 1)
                if k >= 4:
                    dve.wait_ge(pv_mm, k - 3)
                nc.vector.tensor_tensor(prt_lo[:, k % 4, :], ps_t[:, k % NB_T, :], prt_hi[:, k % 4, :].bitcast(F32),
                                        ALU.subtract).then_inc(p_lo, 1)

            def pair_sum(m):
                dve.wait_ge(exp_done, 4 * m + 4)
                tiles = slice(2 * m, 2 * m + 2)
                nc.vector.tensor_tensor(den[:, tiles], psumh[:, tiles, 0], psumh[:, tiles, 1], ALU.add).then_inc(den_done, 1)

            def pair_reciprocal(m):
                dve.wait_ge(den_done, m + 1)
                tiles = slice(2 * m, 2 * m + 2)
                nc.vector.reciprocal(rden[:, tiles], den[:, tiles]).then_inc(rden_done, 1)

            def pair_residual(m):
                dve.wait_ge(rden_done, m + 1)
                dve.wait_ge(ot_turned, m + 1)
                bank = bank_of[stage_bank["out", m]]
                for t in range(2):
                    i = 2 * m + t
                    ins = nc.vector.scalar_tensor_tensor(h1[:, i, :], bank[:, t * D:(t + 1) * D], rden[:, i:i + 1],
                                                         h0[:, i, :], ALU.mult, ALU.add)
                ins.then_inc(h1_done, 1)

            def pair_stats(m):
                dve.wait_ge(h1_done, m + 1)
                for t in range(2):
                    ins = nc.vector.bn_stats(stats2[:, 2 * m + t, :], h1[:, 2 * m + t, :])
                ins.then_inc(stats2_done, 1)

            def pair_moments(m):
                dve.wait_ge(stats2_done, m + 1)
                for t in range(2):
                    ins = nc.vector.bn_aggr(mv2[:, 2 * m + t, :], stats2[:, 2 * m + t, :])
                ins.then_inc(mv2_ready, 1)

            def late_var(i):
                m = LATE + i
                dve.wait_ge(mv2_ready, m + 1)
                nc.vector.tensor_scalar(rs_late[:, 0, :], mv2[:, 2 * m:2 * m + 2, 1], EPS, None, ALU.add
                                        ).then_inc(var2_ready, 1)

            def late_rsqrt(i):
                m = LATE + i
                tiles = slice(2 * m, 2 * m + 2)
                var, near, t, u = (rs_late[:, r, :] for r in range(4))
                dve.wait_ge(std2_ready, i + 1)
                then_own(nc.vector.reciprocal(near, std2[:, :]))
                then_own(newton_1(t, near, var))
                then_own(newton_2(u, t, near))
                then_own(newton_3(rstd2[:, tiles], u, near))
                nc.vector.scalar_tensor_tensor(shift2[:, :], mv2[:, tiles, 0], -1.0, rstd2[:, tiles],
                                               ALU.mult, ALU.mult).then_inc(rstd2_ready, 1)

            def late_lo(i):
                m = LATE + i
                here = slice(2 * m % CH, 2 * m % CH + 2)
                dve.wait_ge(xn2_hi_ready, i + 1)
                nc.vector.tensor_tensor(xn2_split[:, here, D:2 * D], xn2[:, here, :],
                                        xn2_split[:, here, 0:D].bitcast(F32), ALU.subtract).then_inc(late_xs_ready, 1)

            def expert(g, j):
                t0, n = GROUPS[g]
                w = n * P
                cols = hid_cols(g)
                if j == 1:
                    dve.wait_ge(logit_mm, g + 1)
                    nc.vector.tensor_tensor(logit[:, 0:n, :],
                                            f_bank(g, j)[:, 0:n * E].rearrange("p (t e) -> p t e", e=E),
                                            rb_all[:, :].unsqueeze(1).to_broadcast([P, n, E]), ALU.add
                                            ).then_inc(logit_read, 1)
                elif 3 <= j <= 6 and g >= LATE_HID:
                    b = j - 3
                    dve.wait_ge(hid_ready, NB * g + b + 1)
                    if g >= 1:
                        dve.wait_ge(out_mm, g if g < TAIL else g - 1)
                    then_own(nc.vector.tensor_copy(hid_part[:, b, 0, cols], hid[:, b, 0:w]))
                    nc.vector.tensor_tensor(hid_part[:, b, 1, cols], hid[:, b, 0:w], hid_part[:, b, 0, cols].bitcast(F32),
                                            ALU.subtract).then_inc(hid_lo_ready, 1)
                elif j == 8:
                    dve.wait_ge(out_turned, g + 1)
                    nc.vector.scalar_tensor_tensor(res[:, t0:t0 + n, :], f_bank(g, j)[:, 0:n * D].rearrange("p (t d) -> p t d", d=D),
                                                   0.0, h1[:, t0:t0 + n, :], ALU.max, ALU.add).then_inc(res_done, 1)

            def choose(g, step):
                t0, n = GROUPS[g]
                lg, ti, ch = logit[:, 0:n, :], tie[:, 0:n, :], chosen[:, 0:n, :]
                if step == 0:
                    dve.wait_ge(logit_read, g + 1)
                    ins = nc.vector.tensor_reduce(lmax[:, 0:n], lg, AX.X, ALU.max)
                else:
                    dve.wait_ge(choose_step, 3 * g + step)
                if step == 1:
                    for t in range(n):
                        ins = nc.vector.scalar_tensor_tensor(tie[:, t, :], logit[:, t, :], lmax[:, t:t + 1], rev,
                                                             ALU.is_equal, ALU.mult)
                elif step == 2:
                    ins = nc.vector.tensor_reduce(tmax[:, 0:n], ti, AX.X, ALU.max)
                if step < 3:
                    ins.then_inc(choose_step, 1)
                else:
                    nc.vector.tensor_tensor(ch, ti, tmax[:, 0:n].unsqueeze(2).to_broadcast([P, n, E]),
                                            ALU.is_equal).then_inc(chosen_ready, 1)

            for k in slots:
                if k in late_q:
                    split_q(late_q[k])
                for g, step in choices.get(k, []):
                    choose(g, step)
                u = k + LAG
                if EARLY <= u < 4 * NT:
                    add_bias(u)
                    if u % 4 == 3:
                        half_max(u // 4)
                if 0 <= k < 4 * NT:
                    copy_lo(k)
                if 0 <= u < 4 * NT and u % 4 == 3:
                    row_max(u // 4)
                for at, step in zip(PAIR_AT, (pair_sum, pair_reciprocal, pair_residual, pair_stats, pair_moments)):
                    if (k - at) % 8 == 0 and 0 <= (k - at) // 8 < NPAIR:
                        step((k - at) // 8)
                for i, slots_of in enumerate(LATE_SLOTS):
                    for step, at in zip((late_var, late_rsqrt, late_lo), slots_of):
                        if k == at:
                            step(i)
                for g, j in dve_stages.get(k, []):
                    expert(g, j)


def layouts(given):
    w = {name.replace("L0_attn_", "").replace("L0_ffn_", ""): np.asarray(a) for name, a in given.items()}
    w1_d = w["W1"].transpose(1, 0, 2).reshape(D, E * H)
    w2_h = w["W2"].reshape(NB, P, D).transpose(1, 0, 2).reshape(P, NB * D)
    return {
        "x": w["x"], "tok_w": w["L0_tok_W"],
        "w_qkv": np.concatenate([w["Wq"], w["Wq"], w["Wk"], w["Wk"], w["Wv"], w["Wv"]], axis=1),
        "b_rows": np.concatenate([w["bq"], w["bq"], w["bk"], w["bk"], w["b1"].reshape(-1)]).reshape(2 + NB, P),
        "bv": w["bv"], "beta": w["beta"],
        "rw": np.concatenate([w["router_w"], w["router_w"]], axis=1), "rb": w["router_b"],
        "w1_d": np.concatenate([w1_d, w1_d], axis=0), "w2_h": w2_h, "b2": w["b2"],
    }


def kernel(**inputs):
    import numpy as _np
    import concourse.bacc as _bacc
    from concourse import mybir as _mybir
    from concourse.bass_utils import run_bass_kernel_spmd as _run

    nc = _bacc.Bacc("TRN2", target_bir_lowering=False, num_devices=1)
    arrays, args = {}, []
    for name, a in {**layouts(inputs), **tables()}.items():
        arrays[f"in_{name}"] = _np.ascontiguousarray(a)
        args.append(nc.dram_tensor(f"in_{name}", a.shape, _mybir.dt.from_np(a.dtype), kind="ExternalInput").ap())
    args.append(nc.dram_tensor("out_0", (1, S, D), _mybir.dt.float32, kind="ExternalOutput").ap())
    build(nc, *args)
    r = _run(nc, [arrays], core_ids=[0])
    return r.results[0]["out_0"]
```
